# Optimizing a Trainium2 kernel written in Bass

```python
import numpy as np
import jax
import jax.numpy as jnp

def _softmax(x, axis=-1):
    return jax.nn.softmax(x, axis=axis)

def _gelu(x):
    return jax.nn.gelu(x, approximate=True)

def _silu(x):
    return jax.nn.silu(x)

def _sigmoid(x):
    return jax.nn.sigmoid(x)

def _layernorm(x, axis=-1, eps=1e-05):
    m = jnp.mean(x, axis=axis, keepdims=True)
    v = jnp.var(x, axis=axis, keepdims=True)
    return (x - m) / jnp.sqrt(v + eps)

def _scatter_add(tgt, idx, src, axis=0):
    return tgt.at[idx].add(src)

def _segment_sum(src, seg, n):
    return jax.ops.segment_sum(src, seg, n)
kernel_name = 'mk_vit_tower_postln_d1_tok_img768_r4_305197'

def setup_inputs(seed: int=0):
    np.random.seed(seed)
    _w = jnp.asarray

    def _rec_inputs():
        import jax
        import jax.numpy as jnp
        _rk = jax.random.key(seed)
        x = -0.000356955 + 1 * jax.random.normal(jax.random.fold_in(_rk, 1), (32, 3, 96, 96), jnp.float32)
        return x
    x = _rec_inputs()

    def _L0_tok_setup():
        import jax, jax.numpy as jnp
        import numpy as np
        PATCH = 16
        EPS = 1e-06

        def _layernorm(x, gamma, beta, eps=EPS):
            mu = jnp.mean(x, axis=-1, keepdims=True)
            var = jnp.var(x, axis=-1, keepdims=True)
            return (x - mu) * jax.lax.rsqrt(var + eps) * gamma + beta
        key = jax.random.key(seed)
        k_x, k_w = jax.random.split(key)
        B, C, H, W = (128, 3, 224, 224)
        patch_dim = C * PATCH * PATCH
        embed_dim = 192
        x = jax.random.normal(k_x, (B, C, H, W), dtype=jnp.float32)
        W_proj = jax.random.normal(k_w, (patch_dim, embed_dim), dtype=jnp.float32) * (1.0 / np.sqrt(patch_dim))
        ln1_g = jnp.ones((patch_dim,), jnp.float32)
        ln1_b = jnp.zeros((patch_dim,), jnp.float32)
        ln2_g = jnp.ones((embed_dim,), jnp.float32)
        ln2_b = jnp.zeros((embed_dim,), jnp.float32)
        return {'x': x, 'W_proj': W_proj, 'ln1_g': ln1_g, 'ln1_b': ln1_b, 'ln2_g': ln2_g, 'ln2_b': ln2_b}
    _L0_tok_all = _L0_tok_setup()
    _L0_tok_in = {k: v for k, v in _L0_tok_all.items() if k in ('W_proj', 'ln1_g', 'ln1_b', 'ln2_g', 'ln2_b')}
    del _L0_tok_all

    def _L0_attn_setup():
        import jax, jax.numpy as jnp
        import numpy as np
        B, N, C, H = (8, 1024, 192, 8)
        key = jax.random.key(seed)
        k1, k2, k3 = jax.random.split(key, 3)
        x = jax.random.normal(k1, (B, N, C), dtype=jnp.float32)
        W_qkv = jax.random.normal(k2, (C, 3 * C), dtype=jnp.float32) * 0.02
        W_proj = jax.random.normal(k3, (C, C), dtype=jnp.float32) * 0.02
        b_proj = jnp.zeros((C,), dtype=jnp.float32)
        temp = jnp.ones((H, 1, 1), dtype=jnp.float32)
        return {'x': x, 'W_qkv': W_qkv, 'W_proj': W_proj, 'b_proj': b_proj, 'temp': temp}
    _L0_attn_all = _L0_attn_setup()
    _L0_attn_in = {k: v for k, v in _L0_attn_all.items() if k in ('W_qkv', 'W_proj', 'b_proj', 'temp')}
    del _L0_attn_all

    def _L0_ffn_setup():
        import jax, jax.numpy as jnp
        import numpy as np
        EPS = 1e-06

        def l2_normalize(x, axis):
            norm = jnp.sqrt(jnp.square(x).sum(axis=axis, keepdims=True))
            return x * (1.0 / (norm + EPS))
        key = jax.random.key(seed)
        ks = jax.random.split(key, 8)
        b, m, d = (32, 256, 192)
        n, p = (8, 4)
        h = d // 8
        X = jax.random.normal(ks[0], (b, m, d), dtype=jnp.float32)
        std_slot = float(np.sqrt(2.0 / (d + n * p)))
        slot_params = jax.random.normal(ks[1], (d, n, p), dtype=jnp.float32) * std_slot
        scale = jnp.ones((), dtype=jnp.float32)
        W_down = jax.random.normal(ks[2], (n, d, h), dtype=jnp.float32) * float(np.sqrt(1.0 / d))
        b_down = jnp.zeros((n, h), dtype=jnp.float32)
        W_up = jax.random.normal(ks[3], (n, h, d), dtype=jnp.float32) * float(np.sqrt(1.0 / h))
        b_up = jnp.zeros((n, d), dtype=jnp.float32)
        return {'X': X, 'slot_params': slot_params, 'scale': scale, 'W_down': W_down, 'b_down': b_down, 'W_up': W_up, 'b_up': b_up}
    _L0_ffn_all = _L0_ffn_setup()
    _L0_ffn_in = {k: v for k, v in _L0_ffn_all.items() if k in ('slot_params', 'scale', 'W_down', 'b_down', 'W_up', 'b_up')}
    del _L0_ffn_all
    return {'x': x, 'L0_tok_W_proj': _L0_tok_in['W_proj'], 'L0_tok_ln1_g': _L0_tok_in['ln1_g'], 'L0_tok_ln1_b': _L0_tok_in['ln1_b'], 'L0_tok_ln2_g': _L0_tok_in['ln2_g'], 'L0_tok_ln2_b': _L0_tok_in['ln2_b'], 'L0_attn_W_qkv': _L0_attn_in['W_qkv'], 'L0_attn_W_proj': _L0_attn_in['W_proj'], 'L0_attn_b_proj': _L0_attn_in['b_proj'], 'L0_attn_temp': _L0_attn_in['temp'], 'L0_ffn_slot_params': _L0_ffn_in['slot_params'], 'L0_ffn_scale': _L0_ffn_in['scale'], 'L0_ffn_W_down': _L0_ffn_in['W_down'], 'L0_ffn_b_down': _L0_ffn_in['b_down'], 'L0_ffn_W_up': _L0_ffn_in['W_up'], 'L0_ffn_b_up': _L0_ffn_in['b_up']}

def reference(x, L0_tok_W_proj, L0_tok_ln1_g, L0_tok_ln1_b, L0_tok_ln2_g, L0_tok_ln2_b, L0_attn_W_qkv, L0_attn_W_proj, L0_attn_b_proj, L0_attn_temp, L0_ffn_slot_params, L0_ffn_scale, L0_ffn_W_down, L0_ffn_b_down, L0_ffn_W_up, L0_ffn_b_up):
    import jax
    import jax.numpy as jnp

    def _L0_tok_ref(x, W_proj, ln1_g, ln1_b, ln2_g, ln2_b):
        import jax, jax.numpy as jnp
        import numpy as np
        PATCH = 16
        EPS = 1e-06

        def _layernorm(x, gamma, beta, eps=EPS):
            mu = jnp.mean(x, axis=-1, keepdims=True)
            var = jnp.var(x, axis=-1, keepdims=True)
            return (x - mu) * jax.lax.rsqrt(var + eps) * gamma + beta
        B, C, H, W = x.shape
        h, w = (H // PATCH, W // PATCH)
        p = x.reshape(B, C, h, PATCH, w, PATCH)
        p = p.transpose(0, 2, 4, 3, 5, 1)
        p = p.reshape(B, h * w, PATCH * PATCH * C)
        p = _layernorm(p, ln1_g, ln1_b)
        y = jnp.einsum('bnd,de->bne', p, W_proj)
        return _layernorm(y, ln2_g, ln2_b)

    def _L0_attn_ref(x, W_qkv, W_proj, b_proj, temp):
        import jax, jax.numpy as jnp
        import numpy as np
        B, N, C, H = (8, 1024, 192, 8)
        b, n, c = x.shape
        h = temp.shape[0]
        d = c // h
        qkv = (x @ W_qkv).reshape(b, n, h, d, 3)
        q, k, v = (qkv[..., 0], qkv[..., 1], qkv[..., 2])
        q = q / jnp.linalg.norm(q, axis=1, keepdims=True)
        k = k / jnp.linalg.norm(k, axis=1, keepdims=True)
        attn = jnp.einsum('bnhd,bnhe->bhde', q, k) * temp
        attn = jax.nn.softmax(attn, axis=-1)
        y = jnp.einsum('bhde,bnhe->bnhd', attn, v).reshape(b, n, c)
        return y @ W_proj + b_proj

    def _L0_ffn_ref(X, slot_params, scale, W_down, b_down, W_up, b_up):
        import jax, jax.numpy as jnp
        import numpy as np
        EPS = 1e-06

        def l2_normalize(x, axis):
            norm = jnp.sqrt(jnp.square(x).sum(axis=axis, keepdims=True))
            return x * (1.0 / (norm + EPS))
        b, m, d = X.shape
        _, n, p = slot_params.shape
        Xn = l2_normalize(X, axis=-1)
        sp = l2_normalize(slot_params, axis=1) * scale
        logits = jnp.einsum('bmd,dnp->bmnp', Xn, sp)
        D = jax.nn.softmax(logits, axis=1)
        C = jax.nn.softmax(logits.reshape(b, m, n * p), axis=2).reshape(b, m, n, p)
        X_tilde = jnp.einsum('bmd,bmnp->bnpd', Xn, D)
        H = jax.nn.gelu(jnp.einsum('bnpd,ndh->bnph', X_tilde, W_down) + b_down[None, :, None, :], approximate=False)
        Y_tilde = jnp.einsum('bnph,nhd->bnpd', H, W_up) + b_up[None, :, None, :]
        Y = jnp.einsum('bnpd,bmnp->bmd', Y_tilde, C)
        return Y
    h = _L0_tok_ref(x, L0_tok_W_proj, L0_tok_ln1_g, L0_tok_ln1_b, L0_tok_ln2_g, L0_tok_ln2_b)
    h = _layernorm(h + _L0_attn_ref(h, L0_attn_W_qkv, L0_attn_W_proj, L0_attn_b_proj, L0_attn_temp), axis=-1)
    h = _layernorm(h + _L0_ffn_ref(h, L0_ffn_slot_params, L0_ffn_scale, L0_ffn_W_down, L0_ffn_b_down, L0_ffn_W_up, L0_ffn_b_up), axis=-1)
    return h

_drawn_inputs = setup_inputs


def setup_inputs(seed=0):
    import zlib

    import numpy as np

    out = dict(_drawn_inputs(seed))
    spreads = {'L0_tok_ln1_g': (1.0, 0.2),
     'L0_tok_ln1_b': (0.0, 0.1),
     'L0_tok_ln2_g': (1.0, 0.2),
     'L0_tok_ln2_b': (0.0, 0.1),
     'L0_attn_b_proj': (0.0, 0.1),
     'L0_attn_temp': (1.0, 0.6),
     'L0_ffn_b_down': (0.0, 0.421),
     'L0_ffn_b_up': (0.0, 0.1)}
    factors = {'L0_attn_W_qkv': 3.573,
     'L0_attn_W_proj': 3.691,
     'L0_ffn_slot_params': 8.0,
     'L0_ffn_W_down': 8.0,
     'L0_ffn_W_up': 3.017}
    for name, (base, spread) in spreads.items():
        noise = np.random.default_rng([zlib.crc32(name.encode()), seed]).standard_normal(out[name].shape)
        drawn = base * np.exp(spread * noise) if base else spread * noise
        out[name] = jnp.asarray(drawn.astype(out[name].dtype))
    for name, factor in factors.items():
        out[name] = (out[name] * factor).astype(out[name].dtype)
    return out
```

```python
from contextlib import ExitStack

import numpy as np

import concourse.bass as bass
from concourse import mybir

F32 = mybir.dt.float32
ACT = mybir.ActivationFunctionType
ALU = mybir.AluOpType
AX = mybir.AxisListType

B, CH, IMG, PATCH = 32, 3, 96, 16
SIDE = IMG // PATCH
TOK = SIDE * SIDE
NTOK = B * TOK
D = 192
HEADS, DH = 8, D // 8
PD = CH * PATCH * PATCH
KC = PD // 128
GI = 3
NG = (B + GI - 1) // GI
F = D // 2
NE, NP = 8, 4
SL = NE * NP
HID = D // 8
HB = ((0, 4), (4, 8), (8, NG))
NEG = -1.0e30
EPS_TOK, EPS_LN, EPS_L2 = 1e-6, 1e-5, 1e-6


def images(g):
    return min(GI, B - g * GI)


def tokens(g):
    return images(g) * TOK


def build(nc, x, x_t, w_tok, ln1_g, ln1_b, ln2_g, ln2_b, g2col, b2col, w_qkv, w_proj, b_proj, temp, slots, scale,
          w_down, b_down, w_up, b_up, ident_h, imgsel_h, negmask_h, pads_h, out):
    ctx = ExitStack()
    with ctx:
        def sb(name, shape):
            return ctx.enter_context(nc.sbuf_tensor(name, shape, F32))

        def sem(name):
            return ctx.enter_context(nc.semaphore(name))

        ident = sb("ident", [128, 128])
        imgsel = sb("imgsel", [128, GI])
        negmask = sb("negmask", [128, GI * SL])
        pads = sb("pads", [128, 2])
        g1 = sb("g1", [128, KC])
        b1 = sb("b1", [128, KC])
        wt = sb("wt", [128, KC, D])
        wg = sb("wg", [128, KC, D])
        wc = sb("wc", [128, KC, D])
        bw = sb("bw", [128, D])
        share = sb("share", [128, 128])
        g2 = sb("g2", [F, 2])
        b2 = sb("b2", [F, 2])
        g2row = sb("g2row", [128, D])
        b2row = sb("b2row", [128, D])
        bprow = sb("bprow", [128, D])
        wraw = sb("wraw", [F, 2, HEADS, DH, 3])
        wqk = sb("wqk", [F, 2, 2, HEADS, DH])
        wv = sb("wv", [F, 2, HEADS, 32])
        wp = sb("wp", [F, 2, D])
        tempc = sb("tempc", [128, 2])
        spraw = sb("spraw", [F, 2, NE, NP])
        spsq = sb("spsq", [F, 2, NE, NP])
        spn = sb("spn", [F, 2, NP])
        spe = sb("spe", [F, 2, NP])
        sp3 = sb("sp3", [F, 2, GI, NE, NP])
        scl = sb("scl", [F, 1])
        wd = sb("wd", [F, 2, NE, HID])
        bd = sb("bd", [128, 2])
        wu = sb("wu", [128, 2, D])
        bu = sb("bu", [GI * SL, D])
        mhalf = sb("mhalf", [128, 12])
        phalf = sb("phalf", [128, 8])

        NB = 4
        xs = sb("xs", [128, NB, PD])
        st1 = sb("st1", [128, 2, 2, 6])
        mv1 = sb("mv1", [128, NG, 2])
        var1 = sb("var1", [128, NG])
        rstd1 = sb("rstd1", [128, NG])
        y1 = sb("y1", [128, NB, D])
        xT = sb("xT", [128, KC * NTOK])
        st2 = sb("st2", [128, 2, 6])
        mv2 = sb("mv2", [128, NG, 2])
        var2 = sb("var2", [128, NG])
        rstd2 = sb("rstd2", [128, NG])
        NN = 4
        n2 = sb("n2", [128, NN, D])
        z = sb("z", [128, NG, D])
        hT = sb("hT", [F, 2, NTOK])
        NK = 3
        kp = sb("kp", [128, NK, HEADS, 32])
        qm = sb("qm", [128, NK, GI, D])
        sq = sb("sq", [128, 2, 2, HEADS, 32])
        nsq = sb("nsq", [128, NG, 4, GI])
        rn = sb("rn", [128, NG, 4, GI])
        rqt = sb("rqt", [128, NG, 2, GI])
        NS = 4
        e1 = sb("e1", [128, NS, 2, GI, 32])
        e2 = sb("e2", [128, NS, 2, GI, 32])
        mx = sb("mx", [128, NS, 2, GI])
        pr = sb("pr", [128, NS, 2, GI, 32])
        PTW = 3 * DH + 32
        pt = sb("pt", [128, NS, 2 * GI, PTW])
        vT = sb("vT", [128, 2, B, TOK + 1])
        NY = 3
        rden = sb("rden", [F, NY, 2, GI])
        yT = sb("yT", [F, NY, 2, GI, TOK])
        st3 = sb("st3", [128, 2, 6])
        mv3 = sb("mv3", [128, NG, 2])
        pw3 = sb("pw3", [128, NG, 2])
        r3 = sb("r3", [128, NG, 2])
        nrm3 = sb("nrm3", [128, NG])
        inv3 = sb("inv3", [128, NG])
        xn = sb("xn", [128, NG, D])
        NX = 3
        xnT = sb("xnT", [F, NX, 2, GI * TOK])
        lm = sb("lm", [128, NX, GI * SL])
        mC = sb("mC", [128, NX])
        mD = sb("mD", [128, NX])
        eC = sb("eC", [128, NX, GI * SL])
        eD = sb("eD", [128, NX, GI * TOK])
        sC = sb("sC", [128, NG])
        sD = sb("sD", [128, NG])
        rC = sb("rC", [128, NG])
        rD = sb("rD", [128, NG])
        dm = sb("dm", [128, NX, GI * SL])
        cT = sb("cT", [GI * SL, NG, GI * TOK])
        xt = sb("xt", [F, 2, B, NE, NP])
        hb = sb("hb", [128, 2, B, NE, NP])
        NQ = 3
        yt = sb("yt", [GI * SL, NQ, D])
        z2 = sb("z2", [128, NQ, D])
        st4 = sb("st4", [128, 2, 6])
        mv4 = sb("mv4", [128, NG, 2])
        var4 = sb("var4", [128, NG])
        rstd4 = sb("rstd4", [128, NG])
        o4 = sb("o4", [128, NQ, D])

        ps = ctx.enter_context(nc.psum_tensor("ps", [128, 8, 512], F32))

        def csp():
            return ps[:, 4, 0:D]

        def bwp():
            return ps[:, 5, 0:D]

        def tokp(g):
            return ps[0:tokens(g), g % 4, 0:D]

        def htp(g):
            return ps[0:F, 6 + g % 2, 0:2 * GI * TOK].rearrange("p (f n) -> p f n", f=2)[:, :, 0:tokens(g)]

        def qkp(g):
            return ps[0:tokens(g), g % 2, 0:2 * D]

        def nrmp(g):
            return ps[:, 2, 0:4 * GI].rearrange("p (j i) -> p j i", j=4)[:, :, 0:images(g)]

        def gramp(g):
            return ps[:, 3:5, 0:GI * F].rearrange("p b (i c) -> p b i c", i=GI)

        def vp(g):
            return ps[:, 5, 0:2 * GI * TOK].rearrange("p (m n) -> p m n", m=2)[:, :, 0:tokens(g)]

        def yp(g):
            return ps[0:F, 6, 0:2 * GI * (TOK + 1)].rearrange("p (m i n) -> p m i n", m=2, i=GI)

        def prp(g):
            return ps[0:tokens(g), 7, 0:D]

        def xntp(g):
            return ps[0:F, g % 2, 0:2 * GI * TOK].rearrange("p (f n) -> p f n", f=2)[:, :, 0:tokens(g)]

        def lgp(g):
            return ps[0:tokens(g), 2, 0:images(g) * SL]

        def ltp(g):
            return ps[0:images(g) * SL, 3, 0:tokens(g)]

        def dp(g):
            return ps[0:tokens(g), 4 + g % 2, 0:images(g) * SL]

        def cp(g):
            return ps[0:images(g) * SL, 4 + g % 2, 128:128 + tokens(g)]

        def xtlp(g):
            return ps[0:F, 6 + g % 2, 0:2 * GI * SL].rearrange("p (f s) -> p f s", f=2)[:, :, 0:images(g) * SL]

        def hp(b, ni):
            return ps[:, b % 2, 0:2 * ni * NP].rearrange("p (e i s) -> p e i s", e=2, i=ni)

        def ytp(g):
            return ps[0:images(g) * SL, 2 + g % 2, 0:D]

        def yop(g):
            return ps[0:tokens(g), 4 + g % 2, 0:D]

        x_in = [sem(f"x_in{g}") for g in range(NG)]
        xT_in = [sem(f"xT_in{g}") for g in range(NG)]
        ident_in = sem("ident_in")
        ln1_in = sem("ln1_in")
        wtok_in = sem("wtok_in")
        ln2_in = sem("ln2_in")
        wqkv_in = sem("wqkv_in")
        rows_in = sem("rows_in")
        masks_in = sem("masks_in")
        attn_in = sem("attn_in")
        slots_in = sem("slots_in")
        experts_in = sem("experts_in")
        out_done = [sem(f"out_done{i}") for i in range(NQ)]
        cleared = sem("cleared")
        wqk_ready = sem("wqk_ready")
        wv_ready = sem("wv_ready")
        rowsum_ready = sem("rowsum_ready")
        sp_sq = sem("sp_sq")
        sp_sum = sem("sp_sum")
        sp_root = sem("sp_root")
        sp_eps = sem("sp_eps")
        sp_inv = sem("sp_inv")
        sp_scaled = sem("sp_scaled")
        sp_ready = sem("sp_ready")
        share_set = sem("share_set")
        wg_ready = sem("wg_ready")
        csp_ready = sem("csp_ready")
        wc_ready = sem("wc_ready")
        bwp_ready = sem("bwp_ready")
        bw_ready = sem("bw_ready")
        st1_ready = sem("st1_ready")
        mv1_ready = sem("mv1_ready")
        var1_ready = sem("var1_ready")
        rstd1_ready = sem("rstd1_ready")
        y1_ready = sem("y1_ready")
        tokp_ready = sem("tokp_ready")
        st2_ready = sem("st2_ready")
        mv2_ready = sem("mv2_ready")
        var2_ready = sem("var2_ready")
        rstd2_ready = sem("rstd2_ready")
        n_ready = sem("n_ready")
        htp_ready = sem("htp_ready")
        hT_ready = sem("hT_ready")
        rmul_ready = sem("rmul_ready")
        r_ready = sem("r_ready")
        qkp_ready = sem("qkp_ready")
        sq_ready = sem("sq_ready")
        qk_ready = sem("qk_ready")
        nrmp_ready = sem("nrmp_ready")
        nsq_ready = sem("nsq_ready")
        rn_ready = sem("rn_ready")
        rqt_ready = sem("rqt_ready")
        gramp_ready = sem("gramp_ready")
        e1_ready = sem("e1_ready")
        e1_turned = sem("e1_turned")
        e2_scaled = sem("e2_scaled")
        mx_ready = sem("mx_ready")
        e2_ready = sem("e2_ready")
        pr_ready = sem("pr_ready")
        pt_ready = sem("pt_ready")
        vp_ready = sem("vp_ready")
        v_ready = sem("v_ready")
        yp_ready = sem("yp_ready")
        rden_ready = sem("rden_ready")
        y_ready = sem("y_ready")
        prp_ready = sem("prp_ready")
        z_ready = sem("z_ready")
        st3_ready = sem("st3_ready")
        mv3_ready = sem("mv3_ready")
        pw3_ready = sem("pw3_ready")
        r3_ready = sem("r3_ready")
        nrm3_ready = sem("nrm3_ready")
        h1_ready = sem("h1_ready")
        xn_ready = sem("xn_ready")
        xntp_ready = sem("xntp_ready")
        xnT_ready = sem("xnT_ready")
        lgp_ready = sem("lgp_ready")
        lm_ready = sem("lm_ready")
        mC_ready = sem("mC_ready")
        ltp_ready = sem("ltp_ready")
        mD_ready = sem("mD_ready")
        eC_ready = sem("eC_ready")
        eD_ready = sem("eD_ready")
        rD_ready = sem("rD_ready")
        eD_scaled = sem("eD_scaled")
        dcp_ready = sem("dcp_ready")
        dm_ready = sem("dm_ready")
        cT_ready = sem("cT_ready")
        xtlp_ready = sem("xtlp_ready")
        xt_ready = sem("xt_ready")
        hp_ready = sem("hp_ready")
        hb_ready = sem("hb_ready")
        ytp_ready = sem("ytp_ready")
        yt_ready = sem("yt_ready")
        yop_ready = sem("yop_ready")
        z2_ready = sem("z2_ready")
        st4_ready = sem("st4_ready")
        mv4_ready = sem("mv4_ready")
        var4_ready = sem("var4_ready")
        rstd4_ready = sem("rstd4_ready")
        o4_ready = sem("o4_ready")

        block = ctx.enter_context(nc.Block())

        @block.sync
        def _(sp):
            def load_x(g):
                n = tokens(g)
                o = g * GI * TOK * KC
                sp.dma_start(xT[:, o:o + KC * n], x_t[:, o:o + KC * n]).then_inc(xT_in[g], 16)
                if g >= NB:
                    sp.wait_ge(st1_ready, g - NB + 1)
                sp.dma_start(xs[0:n, g % NB, :], x[g * GI * TOK:g * GI * TOK + n, :]).then_inc(x_in[g], 16)

            sp.dma_start(g1[:, :], ln1_g).then_inc(ln1_in, 16)
            sp.dma_start(b1[:, :], ln1_b).then_inc(ln1_in, 16)
            sp.dma_start(wt[:, :, :], w_tok.rearrange("(k p) e -> p k e", p=128)).then_inc(wtok_in, 16)
            load_x(0)
            sp.dma_start(ident[:, :], ident_h).then_inc(ident_in, 16)
            load_x(1)
            load_x(2)
            sp.dma_start(g2[:, :], g2col).then_inc(ln2_in, 16)
            sp.dma_start(b2[:, :], b2col).then_inc(ln2_in, 16)
            sp.dma_start(wraw[:, :, :, :, :].rearrange("p f h d j -> p f (h d j)"),
                         w_qkv.rearrange("(f p) n -> p f n", f=2)).then_inc(wqkv_in, 16)
            load_x(3)
            sp.dma_start(g2row[:, :], ln2_g.partition_broadcast(128)).then_inc(rows_in, 16)
            sp.dma_start(b2row[:, :], ln2_b.partition_broadcast(128)).then_inc(rows_in, 16)
            sp.dma_start(bprow[:, :], b_proj.partition_broadcast(128)).then_inc(rows_in, 16)
            sp.dma_start(imgsel[:, :], imgsel_h).then_inc(masks_in, 16)
            sp.dma_start(negmask[:, :], negmask_h).then_inc(masks_in, 16)
            sp.dma_start(pads[:, :], pads_h).then_inc(masks_in, 16)
            sp.dma_start(tempc[:, :], temp).then_inc(attn_in, 16)
            sp.dma_start(wp[:, :, :], w_proj.rearrange("(f p) n -> p f n", f=2)).then_inc(attn_in, 16)
            for g in range(4, NG):
                load_x(g)
            sp.dma_start(spraw[:, :, :, :].rearrange("p f n q -> p f (n q)"),
                         slots.rearrange("(f p) n q -> p f (n q)", f=2)).then_inc(slots_in, 16)
            sp.dma_start(scl[:, :], scale.broadcast_to([F, 1])).then_inc(slots_in, 16)
            sp.dma_start(wd[:, :, :, :].rearrange("p f n h -> p f (n h)"), w_down).then_inc(experts_in, 16)
            sp.dma_start(bd[:, :], b_down).then_inc(experts_in, 16)
            sp.dma_start(bu[:, :], b_up).then_inc(experts_in, 16)
            sp.wait_ge(cleared, 8)
            for j in range(4):
                sp.dma_start(wu[32 * j:32 * j + HID, :, :], w_up[j]).then_inc(experts_in, 16)

            ov = out.rearrange("b n d -> (b n) d")
            for g in range(NG):
                sp.wait_ge(o4_ready, g + 1)
                sp.dma_start(ov[g * GI * TOK:g * GI * TOK + tokens(g), :],
                             o4[0:tokens(g), g % NQ, :]).then_inc(out_done[g % NQ], 16)
            for i in range(NQ):
                sp.wait_ge(out_done[i], 16 * len(range(i, NG, NQ)))

        @block.tensor
        def _(pe):
            def offset():
                pe.wait_ge(ln1_in, 32)
                pe.wait_ge(wtok_in, 16)
                for kc in range(KC):
                    mm = pe.matmul(bwp(), b1[:, kc:kc + 1].broadcast_to([128, 128]), wt[:, kc, :],
                                   start=kc == 0, stop=kc == KC - 1)
                mm.then_inc(bwp_ready, 1)

            def column_means():
                pe.wait_ge(share_set, 1)
                for kc in range(KC):
                    pe.wait_ge(wg_ready, kc + 1)
                    mm = pe.matmul(csp(), share[:, :], wg[:, kc, :], start=kc == 0, stop=kc == KC - 1)
                mm.then_inc(csp_ready, 1)

            def token(g):
                n = tokens(g)
                o = g * GI * TOK * KC
                pe.wait_ge(xT_in[g], 16)
                if g >= 4:
                    pe.wait_ge(y1_ready, g - 3)
                for kc in range(KC):
                    mm = pe.matmul(tokp(g), xT[:, o + kc * n:o + (kc + 1) * n], wc[:, kc, :],
                                   start=kc == 0, stop=kc == KC - 1)
                mm.then_inc(tokp_ready, 1)

            def turn_h(g):
                pe.wait_ge(n_ready, g + 1)
                if g >= 2:
                    pe.wait_ge(hT_ready, g - 1)
                for f in range(2):
                    mm = pe.transpose(htp(g)[:, f, :], n2[0:tokens(g), g % NN, f * F:(f + 1) * F],
                                      ident[0:tokens(g), 0:tokens(g)])
                mm.then_inc(htp_ready, 1)

            def qk(g):
                t0 = g * GI * TOK
                pe.wait_ge(hT_ready, g + 1)
                if g >= 2:
                    pe.wait_ge(qk_ready, g - 1)
                for f in range(2):
                    mm = pe.matmul(qkp(g), hT[:, f, t0:t0 + tokens(g)],
                                   wqk[:, f, :, :, :].rearrange("p j h d -> p (j h d)"),
                                   start=f == 0, stop=f == 1)
                mm.then_inc(qkp_ready, 1)

            def norms(g):
                pe.wait_ge(sq_ready, g + 1)
                if g >= 1:
                    pe.wait_ge(nsq_ready, g)
                for j in range(2):
                    for m in range(2):
                        mm = pe.matmul(nrmp(g)[:, 2 * j + m, :],
                                       sq[0:tokens(g), g % 2, j, 4 * m:4 * m + 4, :].rearrange("p h d -> p (h d)"),
                                       imgsel[0:tokens(g), 0:images(g)], start=True, stop=True)
                mm.then_inc(nrmp_ready, 1)

            def gram(g):
                pe.wait_ge(qk_ready, g + 1)
                if g >= 1:
                    pe.wait_ge(e1_ready, g)
                for m in range(2):
                    mm = pe.matmul(gramp(g)[:, m, 0:images(g), :],
                                   kp[0:tokens(g), g % NK, 4 * m:4 * m + 4, :].rearrange("p h d -> p (h d)"),
                                   qm[0:tokens(g), g % NK, 0:images(g), m * F:(m + 1) * F],
                                   start=True, stop=True)
                mm.then_inc(gramp_ready, 1)

            def values(g):
                t0 = g * GI * TOK
                if g >= 1:
                    pe.wait_ge(v_ready, g)
                for m in range(2):
                    for f in range(2):
                        mm = pe.matmul(vp(g)[:, m, :], wv[:, f, 4 * m:4 * m + 4, :].rearrange("p h d -> p (h d)"),
                                       hT[:, f, t0:t0 + tokens(g)], start=f == 0, stop=f == 1)
                mm.then_inc(vp_ready, 1)

            def mix(g):
                pe.wait_ge(pt_ready, g + 1)
                pe.wait_ge(v_ready, g + 1)
                if g >= 1:
                    pe.wait_ge(y_ready, g)
                for m in range(2):
                    for i in range(images(g)):
                        mm = pe.matmul(yp(g)[:, m, i, :], pt[:, g % NS, GI * m + i, 0:F],
                                       vT[:, m, g * GI + i, :], start=True, stop=True)
                mm.then_inc(yp_ready, 1)

            def project(g):
                pe.wait_ge(y_ready, g + 1)
                if g >= 1:
                    pe.wait_ge(z_ready, g)
                for m in range(2):
                    mm = pe.matmul(prp(g), yT[:, g % NY, m, 0:images(g), :].rearrange("p i n -> p (i n)"),
                                   wp[:, m, :], start=m == 0, stop=m == 1)
                mm.then_inc(prp_ready, 1)

            def turn_xn(g):
                pe.wait_ge(xn_ready, g + 1)
                if g >= 2:
                    pe.wait_ge(xnT_ready, g - 1)
                for f in range(2):
                    mm = pe.transpose(xntp(g)[:, f, :], xn[0:tokens(g), g, f * F:(f + 1) * F],
                                      ident[0:tokens(g), 0:tokens(g)])
                mm.then_inc(xntp_ready, 1)

            def logits(g):
                pe.wait_ge(xnT_ready, g + 1)
                if g >= 1:
                    pe.wait_ge(lm_ready, g)
                for f in range(2):
                    mm = pe.matmul(lgp(g), xnT[:, g % NX, f, 0:tokens(g)],
                                   sp3[:, f, 0:images(g), :, :].rearrange("p i n q -> p (i n q)"),
                                   start=f == 0, stop=f == 1)
                mm.then_inc(lgp_ready, 1)

            def turn_l(g):
                pe.wait_ge(lm_ready, g + 1)
                if g >= 1:
                    pe.wait_ge(eD_ready, g)
                pe.transpose(ltp(g), lm[0:tokens(g), g % NX, 0:images(g) * SL],
                             ident[0:tokens(g), 0:tokens(g)]).then_inc(ltp_ready, 1)

            def turn_dc(g):
                n, s = tokens(g), images(g) * SL
                pe.wait_ge(eD_scaled, g + 1)
                pe.wait_ge(eC_ready, g + 1)
                if g >= 2:
                    pe.wait_ge(dm_ready, g - 1)
                    pe.wait_ge(cT_ready, g - 1)
                pe.transpose(dp(g), eD[0:s, g % NX, 0:n], ident[0:s, 0:s])
                pe.transpose(cp(g), eC[0:n, g % NX, 0:s], ident[0:n, 0:n]).then_inc(dcp_ready, 1)

            def slot_in(g):
                pe.wait_ge(dm_ready, g + 1)
                if g >= 2:
                    pe.wait_ge(xt_ready, g - 1)
                for f in range(2):
                    mm = pe.matmul(xtlp(g)[:, f, :], xn[0:tokens(g), g, f * F:(f + 1) * F],
                                   dm[0:tokens(g), g % NX, 0:images(g) * SL], start=True, stop=True)
                mm.then_inc(xtlp_ready, 1)

            def hidden(b):
                i0, i1 = HB[b][0] * GI, min(B, HB[b][1] * GI)
                pe.wait_ge(xt_ready, HB[b][1])
                if b >= 2:
                    pe.wait_ge(hb_ready, b - 1)
                for n in range(NE):
                    j = n % 4
                    for f in range(2):
                        mm = pe.matmul(hp(b, i1 - i0)[32 * j:32 * j + HID, n // 4, :, :], wd[:, f, n, :],
                                       xt[:, f, i0:i1, n, :], start=f == 0, stop=f == 1,
                                       tile_position=(0, 32 * j))
                mm.then_inc(hp_ready, 1)

            def slot_out(g):
                i0, ni = g * GI, images(g)
                pe.wait_ge(hb_ready, 1 + sum(g >= e for _, e in HB[:-1]))
                if g >= 2:
                    pe.wait_ge(yt_ready, g - 1)
                for e in range(2):
                    mm = pe.matmul(ytp(g), hb[:, e, i0:i0 + ni, :, :].rearrange("p i n q -> p (i n q)"),
                                   wu[:, e, :], start=e == 0, stop=e == 1)
                mm.then_inc(ytp_ready, 1)

            def combine(g):
                pe.wait_ge(yt_ready, g + 1)
                pe.wait_ge(cT_ready, g + 1)
                if g >= 2:
                    pe.wait_ge(z2_ready, g - 1)
                pe.matmul(yop(g), cT[0:images(g) * SL, g, 0:tokens(g)], yt[0:images(g) * SL, g % NQ, :],
                          start=True, stop=True).then_inc(yop_ready, 1)

            offset()
            column_means()
            pe.wait_ge(wc_ready, 1)
            for g in range(NG):
                token(g)
                if g == 2:
                    pe.wait_ge(ident_in, 16)
                if g >= 2:
                    turn_h(g - 2)
            pe.wait_ge(wqk_ready, 2)
            pe.wait_ge(wv_ready, 2)
            pe.wait_ge(masks_in, 48)
            pe.wait_ge(y1_ready, NG)
            pe.wait_ge(bw_ready, 1)
            for s in range(NG + 5):
                if s < NG:
                    qk(s)
                if s < 2:
                    turn_h(NG - 2 + s)
                if 1 <= s <= NG:
                    norms(s - 1)
                if s == 2:
                    pe.wait_ge(hT_ready, NG)
                if 2 <= s < NG + 2:
                    values(s - 2)
                    gram(s - 2)
                if 4 <= s < NG + 4:
                    mix(s - 4)
                if s == 5:
                    pe.wait_ge(attn_in, 32)
                if s >= 5:
                    project(s - 5)
            pe.wait_ge(sp_ready, 1)
            pe.wait_ge(qk_ready, NG)
            pe.wait_ge(nsq_ready, NG)
            pe.wait_ge(e1_ready, NG)
            pe.wait_ge(v_ready, NG)
            pe.wait_ge(y_ready, NG)
            for s in range(NG + 4):
                if s < NG:
                    turn_xn(s)
                if 1 <= s <= NG:
                    logits(s - 1)
                if 2 <= s <= NG + 1:
                    turn_l(s - 2)
                if 3 <= s <= NG + 2:
                    turn_dc(s - 3)
                if s == 4:
                    pe.wait_ge(z_ready, NG)
                if s >= 4:
                    slot_in(s - 4)
            pe.wait_ge(experts_in, 16 * (3 + 4))
            pe.wait_ge(xnT_ready, NG)
            hidden(0)
            hidden(1)
            pe.wait_ge(lm_ready, NG)
            pe.wait_ge(eD_ready, NG)
            pe.wait_ge(dm_ready, NG)
            pe.wait_ge(cT_ready, NG)
            for s in range(NG + 1):
                if s == 1:
                    hidden(2)
                if s < NG:
                    slot_out(s)
                if s >= 1:
                    combine(s - 1)

        @block.vector
        def _(dve):
            def token_weights():
                dve.wait_ge(ln1_in, 32)
                dve.wait_ge(wtok_in, 16)
                for kc in range(KC):
                    dve.tensor_scalar(wg[:, kc, :], wt[:, kc, :], g1[:, kc:kc + 1], None,
                                      ALU.mult).then_inc(wg_ready, 1)
                dve.wait_ge(wg_ready, KC)
                dve.wait_ge(csp_ready, 1)
                dve.tensor_tensor(wc[:, :, :], wg[:, :, :], csp().unsqueeze(1).broadcast_to([128, KC, D]),
                                  ALU.subtract).then_inc(wc_ready, 1)
                dve.wait_ge(bwp_ready, 1)
                dve.tensor_copy(bw[:, :], bwp()).then_inc(bw_ready, 1)
                dve.wait_ge(bw_ready, 1)

            def x_stats(g):
                n = tokens(g)
                dve.wait_ge(x_in[g], 16)
                if g >= 2:
                    dve.wait_ge(mv1_ready, g - 1)
                for h in range(2):
                    ins = dve.bn_stats(st1[0:n, g % 2, h, :], xs[0:n, g % NB, h * (PD // 2):(h + 1) * (PD // 2)])
                ins.then_inc(st1_ready, 1)
                dve.wait_ge(st1_ready, g + 1)
                dve.bn_aggr(mv1[0:n, g, :], st1[0:n, g % 2, :, :].rearrange("p h s -> p (h s)")).then_inc(mv1_ready, 1)

            def ln2_stats(g):
                n = tokens(g)
                dve.wait_ge(tokp_ready, g + 1)
                dve.wait_ge(rstd1_ready, g + 1)
                if g >= NB:
                    dve.wait_ge(n_ready, g - NB + 1)
                dve.scalar_tensor_tensor(y1[0:n, g % NB, :], tokp(g), rstd1[0:n, g:g + 1], bw[0:n, :],
                                         ALU.mult, ALU.add).then_inc(y1_ready, 1)
                dve.wait_ge(y1_ready, g + 1)
                if g >= 2:
                    dve.wait_ge(mv2_ready, g - 1)
                dve.bn_stats(st2[0:n, g % 2, :], y1[0:n, g % NB, :]).then_inc(st2_ready, 1)
                dve.wait_ge(st2_ready, g + 1)
                dve.bn_aggr(mv2[0:n, g, :], st2[0:n, g % 2, :]).then_inc(mv2_ready, 1)

            def ln2_norm(g):
                n = tokens(g)
                dve.wait_ge(rstd2_ready, g + 1)
                if g >= NN:
                    dve.wait_ge(htp_ready, g - NN + 1)
                    dve.wait_ge(rmul_ready, g - NN + 1)
                dve.tensor_scalar(n2[0:n, g % NN, :], y1[0:n, g % NB, :], mv2[0:n, g, 0:1],
                                  rstd2[0:n, g:g + 1], ALU.subtract, ALU.mult).then_inc(n_ready, 1)

            def weights():
                dve.wait_ge(wqkv_in, 16)
                for f in range(2):
                    dve.tensor_copy(wqk[:, f, :, :, :],
                                    wraw[:, f, :, :, 0:2].rearrange("p h d j -> p j h d")).then_inc(wqk_ready, 1)
                dve.wait_ge(cleared, 8)
                for f in range(2):
                    dve.tensor_copy(wv[:, f, :, 0:DH], wraw[:, f, :, :, 2]).then_inc(wv_ready, 1)

            def slot_weights():
                dve.wait_ge(slots_in, 32)
                dve.tensor_tensor(spsq[:, :, :, :], spraw[:, :, :, :], spraw[:, :, :, :],
                                  ALU.mult).then_inc(sp_sq, 1)
                dve.wait_ge(sp_sq, 1)
                dve.tensor_reduce(spn[:, :, :], spsq[:, :, :, :].rearrange("p f n q -> p f q n"),
                                  AX.X, ALU.add).then_inc(sp_sum, 1)
                dve.wait_ge(sp_root, 1)
                dve.tensor_scalar(spn[:, :, :], spe[:, :, :], EPS_L2, None, ALU.add).then_inc(sp_eps, 1)
                dve.wait_ge(sp_eps, 1)
                dve.reciprocal(spe[:, :, :], spn[:, :, :]).then_inc(sp_inv, 1)
                dve.wait_ge(sp_inv, 1)
                for f in range(2):
                    ins = dve.tensor_tensor(spsq[:, f, :, :], spraw[:, f, :, :],
                                            spe[:, f, :].unsqueeze(1).broadcast_to([F, NE, NP]), ALU.mult)
                ins.then_inc(sp_scaled, 1)
                dve.wait_ge(sp_scaled, 1)
                for i in range(GI):
                    ins = dve.tensor_scalar(sp3[:, :, i, :, :].rearrange("p f n q -> p f (n q)"),
                                            spsq[:, :, :, :].rearrange("p f n q -> p f (n q)"),
                                            scl[:, 0:1], None, ALU.mult)
                ins.then_inc(sp_ready, 1)

            def norm_sums(g):
                dve.wait_ge(nrmp_ready, g + 1)
                dve.tensor_scalar(nsq[:, g, :, 0:images(g)], nrmp(g), pads[:, 0:1], None,
                                  ALU.add).then_inc(nsq_ready, 1)

            def heads(g):
                ni = images(g)
                dve.wait_ge(gramp_ready, g + 1)
                dve.wait_ge(rn_ready, g + 1)
                if g >= NS:
                    dve.wait_ge(e1_turned, g - NS + 1)
                for j in range(4):
                    r = slice(32 * j, 32 * j + 32)
                    ins = dve.tensor_tensor(
                        e1[r, g % NS, :, 0:ni, 0:DH], gramp(g)[r, :, 0:ni, DH * j:DH * j + DH],
                        rn[r, g, 2:4, 0:ni].unsqueeze(3).broadcast_to([32, 2, ni, DH]), ALU.mult)
                ins.then_inc(e1_ready, 1)

            def rows_e(g):
                ni = images(g)
                s = g % NS
                v = e2[:, s, :, 0:ni, 0:DH]
                dve.wait_ge(e1_ready, g + 1)
                if g >= NS:
                    dve.wait_ge(pr_ready, g - NS + 1)
                dve.transpose(e2[:, s, :, :, :].rearrange("p m i e -> p (m i e)"),
                              e1[:, s, :, :, :].rearrange("p m i e -> p (m i e)")).then_inc(e1_turned, 1)
                dve.wait_ge(e1_turned, g + 1)
                dve.wait_ge(rqt_ready, g + 1)
                dve.tensor_tensor(v, v, rqt[:, g, :, 0:ni].unsqueeze(3).broadcast_to([128, 2, ni, DH]),
                                  ALU.mult).then_inc(e2_scaled, 1)
                dve.wait_ge(e2_scaled, g + 1)
                dve.tensor_reduce(mx[:, s, :, 0:ni], v, AX.X, ALU.max).then_inc(mx_ready, 1)
                dve.wait_ge(mx_ready, g + 1)
                dve.tensor_tensor(v, v, mx[:, s, :, 0:ni].unsqueeze(3).broadcast_to([128, 2, ni, DH]),
                                  ALU.subtract).then_inc(e2_ready, 1)

            def blocks(g):
                s = g % NS
                dve.wait_ge(pr_ready, g + 1)
                if g >= NS:
                    dve.wait_ge(yp_ready, g - NS + 1)
                for j in range(4):
                    r = slice(32 * j, 32 * j + 32)
                    ins = dve.transpose(pt[r, s, :, DH * j:DH * j + 32],
                                        pr[r, s, :, :, :].rearrange("p m i e -> p (m i) e"))
                ins.then_inc(pt_ready, 1)

            def y_norm(g):
                ni = images(g)
                dve.wait_ge(yp_ready, g + 1)
                if g >= NY:
                    dve.wait_ge(prp_ready, g - NY + 1)
                dve.reciprocal(rden[:, g % NY, :, 0:ni], yp(g)[:, :, 0:ni, TOK]).then_inc(rden_ready, 1)
                dve.wait_ge(rden_ready, g + 1)
                dve.tensor_tensor(yT[:, g % NY, :, 0:ni, :], yp(g)[:, :, 0:ni, 0:TOK],
                                  rden[:, g % NY, :, 0:ni].unsqueeze(3).broadcast_to([F, 2, ni, TOK]),
                                  ALU.mult).then_inc(y_ready, 1)

            def residual(g):
                n = tokens(g)
                dve.wait_ge(prp_ready, g + 1)
                dve.wait_ge(r_ready, g + 1)
                dve.tensor_tensor(z[0:n, g, :], prp(g), z[0:n, g, :], ALU.add).then_inc(z_ready, 1)
                dve.wait_ge(z_ready, g + 1)
                dve.bn_stats(st3[0:n, g % 2, :], z[0:n, g, :]).then_inc(st3_ready, 1)
                dve.wait_ge(st3_ready, g + 1)
                dve.bn_aggr(mv3[0:n, g, :], st3[0:n, g % 2, :]).then_inc(mv3_ready, 1)

            def h1(g):
                n = tokens(g)
                dve.wait_ge(r3_ready, g + 1)
                dve.tensor_scalar(nrm3[0:n, g:g + 1], r3[0:n, g, 0:1], r3[0:n, g, 1:2], EPS_L2,
                                  ALU.mult, ALU.add).then_inc(nrm3_ready, 1)
                dve.wait_ge(nrm3_ready, g + 1)
                dve.reciprocal(inv3[0:n, g:g + 1], nrm3[0:n, g:g + 1])
                dve.tensor_scalar(z[0:n, g, :], z[0:n, g, :], mv3[0:n, g, 0:1], r3[0:n, g, 0:1],
                                  ALU.subtract, ALU.mult).then_inc(h1_ready, 1)
                dve.wait_ge(h1_ready, g + 1)
                dve.tensor_scalar(xn[0:n, g, :], z[0:n, g, :], inv3[0:n, g:g + 1], None,
                                  ALU.mult).then_inc(xn_ready, 1)

            def mask_logits(g):
                n, s = tokens(g), images(g) * SL
                dve.wait_ge(lgp_ready, g + 1)
                if g >= NX:
                    dve.wait_ge(eC_ready, g - NX + 1)
                    dve.wait_ge(ltp_ready, g - NX + 1)
                dve.tensor_tensor(lm[0:n, g % NX, 0:s], lgp(g), negmask[0:n, 0:s], ALU.add).then_inc(lm_ready, 1)
                dve.wait_ge(lm_ready, g + 1)
                dve.tensor_reduce(mC[0:n, g % NX:g % NX + 1], lm[0:n, g % NX, 0:s], AX.X, ALU.max,
                                  negate=True).then_inc(mC_ready, 1)

            def max_d(g):
                s = images(g) * SL
                dve.wait_ge(ltp_ready, g + 1)
                if g >= NX:
                    dve.wait_ge(eD_ready, g - NX + 1)
                dve.tensor_reduce(mD[0:s, g % NX:g % NX + 1], ltp(g), AX.X, ALU.max,
                                  negate=True).then_inc(mD_ready, 1)

            def scale_d(g):
                n, s = tokens(g), images(g) * SL
                dve.wait_ge(eD_ready, g + 1)
                dve.wait_ge(eC_ready, g + 1)
                dve.reciprocal(rC[0:n, g:g + 1], sC[0:n, g:g + 1])
                dve.reciprocal(rD[0:s, g:g + 1], sD[0:s, g:g + 1]).then_inc(rD_ready, 1)
                dve.wait_ge(rD_ready, g + 1)
                dve.tensor_scalar(eD[0:s, g % NX, 0:n], eD[0:s, g % NX, 0:n], rD[0:s, g:g + 1], None,
                                  ALU.mult).then_inc(eD_scaled, 1)

            def take_d(g):
                n, s = tokens(g), images(g) * SL
                dve.wait_ge(dcp_ready, g + 1)
                if g >= NX:
                    dve.wait_ge(xtlp_ready, g - NX + 1)
                dve.tensor_copy(dm[0:n, g % NX, 0:s], dp(g)).then_inc(dm_ready, 1)
                dve.tensor_copy(cT[0:s, g, 0:n], cp(g)).then_inc(cT_ready, 1)

            def take_slots(g):
                i0, ni = g * GI, images(g)
                dve.wait_ge(xtlp_ready, g + 1)
                dve.tensor_copy(xt[:, :, i0:i0 + ni, :, :].rearrange("p f i n q -> p f (i n q)"),
                                xtlp(g)).then_inc(xt_ready, 1)

            def slot_bias(g):
                s = images(g) * SL
                dve.wait_ge(ytp_ready, g + 1)
                if g >= NQ:
                    dve.wait_ge(yop_ready, g - NQ + 1)
                dve.tensor_tensor(yt[0:s, g % NQ, :], ytp(g), bu[0:s, :], ALU.add).then_inc(yt_ready, 1)

            def last_residual(g):
                n = tokens(g)
                dve.wait_ge(yop_ready, g + 1)
                dve.scalar_tensor_tensor(z2[0:n, g % NQ, :], yop(g), rC[0:n, g:g + 1], z[0:n, g, :],
                                         ALU.mult, ALU.add).then_inc(z2_ready, 1)
                dve.wait_ge(z2_ready, g + 1)
                dve.bn_stats(st4[0:n, g % 2, :], z2[0:n, g % NQ, :]).then_inc(st4_ready, 1)
                dve.wait_ge(st4_ready, g + 1)
                dve.bn_aggr(mv4[0:n, g, :], st4[0:n, g % 2, :]).then_inc(mv4_ready, 1)

            def last_norm(g):
                n = tokens(g)
                dve.wait_ge(rstd4_ready, g + 1)
                if g >= NQ:
                    dve.wait_ge(out_done[g % NQ], 16 * (g // NQ))
                dve.tensor_scalar(o4[0:n, g % NQ, :], z2[0:n, g % NQ, :], mv4[0:n, g, 0:1],
                                  rstd4[0:n, g:g + 1], ALU.subtract, ALU.mult).then_inc(o4_ready, 1)

            token_weights()
            x_stats(0)
            for s in range(NG + 1):
                if s + 1 < NG:
                    x_stats(s + 1)
                if s < NG:
                    ln2_stats(s)
                if s == 2:
                    weights()
                if s >= 1:
                    ln2_norm(s - 1)
            slot_weights()
            for s in range(1, NG + 7):
                if s <= NG:
                    norm_sums(s - 1)
                if 2 <= s < NG + 2:
                    heads(s - 2)
                    rows_e(s - 2)
                if 3 <= s < NG + 3:
                    blocks(s - 3)
                if 4 <= s < NG + 4:
                    y_norm(s - 4)
                if 5 <= s < NG + 5:
                    residual(s - 5)
                if s >= 6 and s - 6 < NG:
                    h1(s - 6)
            for s in range(NG + 5):
                if s < NG:
                    mask_logits(s)
                if 1 <= s <= NG:
                    max_d(s - 1)
                if 2 <= s <= NG + 1:
                    scale_d(s - 2)
                if 3 <= s <= NG + 2:
                    take_d(s - 3)
                if 4 <= s <= NG + 3:
                    take_slots(s - 4)
            for s in range(NG + 2):
                if s < NG:
                    slot_bias(s)
                if 1 <= s <= NG:
                    last_residual(s - 1)
                if s >= 2:
                    last_norm(s - 2)

        @block.scalar
        def _(act):
            def take_h(g):
                t0 = g * GI * TOK
                act.wait_ge(htp_ready, g + 1)
                for f in range(2):
                    ins = act.activation(hT[:, f, t0:t0 + tokens(g)], htp(g)[:, f, :], ACT.Identity,
                                         bias=b2[:, f:f + 1], scale=g2[:, f:f + 1])
                ins.then_inc(hT_ready, 1)

            def take_qk(g):
                n, ni = tokens(g), images(g)
                act.wait_ge(qkp_ready, g + 1)
                if g >= 2:
                    act.wait_ge(nrmp_ready, g - 1)
                if g >= NK:
                    act.wait_ge(gramp_ready, g - NK + 1)
                p = qkp(g).rearrange("p (j h d) -> p (j h) d", j=2, h=HEADS)
                act.activation(sq[0:n, g % 2, :, :, 0:DH].rearrange("p j h d -> p (j h) d"), p,
                               ACT.Square).then_inc(sq_ready, 1)
                act.activation(kp[0:n, g % NK, :, 0:DH], p[:, HEADS:2 * HEADS, :], ACT.Copy)
                for i in range(ni):
                    ins = act.activation(qm[0:n, g % NK, i, :], qkp(g)[:, 0:D], ACT.Copy,
                                         scale=imgsel[0:n, i:i + 1])
                ins.then_inc(qk_ready, 1)

            def take_v(g):
                i0, ni = g * GI, images(g)
                act.wait_ge(vp_ready, g + 1)
                act.activation(vT[:, :, i0:i0 + ni, 0:TOK], vp(g).rearrange("p m (i n) -> p m i n", i=ni),
                               ACT.Copy).then_inc(v_ready, 1)

            def exp_e(g):
                ni = images(g)
                act.wait_ge(e2_ready, g + 1)
                if g >= NS:
                    act.wait_ge(pt_ready, g - NS + 1)
                act.activation(pr[:, g % NS, :, 0:ni, 0:DH], e2[:, g % NS, :, 0:ni, 0:DH], ACT.Exp,
                               bias=pads[:, 1:2]).then_inc(pr_ready, 1)

            def take_xn(g):
                act.wait_ge(xntp_ready, g + 1)
                if g >= NX:
                    act.wait_ge(lgp_ready, g - NX + 1)
                act.activation(xnT[:, g % NX, :, 0:tokens(g)], xntp(g), ACT.Copy).then_inc(xnT_ready, 1)

            def exp_c(g):
                n, s = tokens(g), images(g) * SL
                act.wait_ge(mC_ready, g + 1)
                if g >= NX:
                    act.wait_ge(dcp_ready, g - NX + 1)
                act.activation(eC[0:n, g % NX, 0:s], lm[0:n, g % NX, 0:s], ACT.Exp,
                               bias=mC[0:n, g % NX:g % NX + 1], accum_out=sC[0:n, g:g + 1]).then_inc(eC_ready, 1)

            def exp_d(g):
                n, s = tokens(g), images(g) * SL
                act.wait_ge(mD_ready, g + 1)
                act.activation(eD[0:s, g % NX, 0:n], ltp(g), ACT.Exp,
                               bias=mD[0:s, g % NX:g % NX + 1], accum_out=sD[0:s, g:g + 1]).then_inc(eD_ready, 1)

            def gelu(b):
                i0, i1 = HB[b][0] * GI, min(B, HB[b][1] * GI)
                act.wait_ge(hp_ready, b + 1)
                for n in range(NE):
                    r = slice(32 * (n % 4), 32 * (n % 4) + HID)
                    ins = act.activation(hb[r, n // 4, i0:i1, n, :], hp(b, i1 - i0)[r, n // 4, :, :],
                                         ACT.Gelu, bias=bd[r, n // 4:n // 4 + 1])
                ins.then_inc(hb_ready, 1)

            act.wait_ge(ln2_in, 32)
            for g in range(NG - 2):
                take_h(g)
            act.wait_ge(masks_in, 48)
            act.wait_ge(cleared, 8)
            for s in range(NG + 3):
                if s < 2:
                    take_h(NG - 2 + s)
                if s < NG:
                    take_qk(s)
                if 2 <= s < NG + 2:
                    take_v(s - 2)
                if s >= 3:
                    exp_e(s - 3)
            for s in range(NG + 2):
                if s < NG:
                    take_xn(s)
                if 1 <= s <= NG:
                    exp_c(s - 1)
                if s >= 2:
                    exp_d(s - 2)
            act.wait_ge(experts_in, 16 * (3 + 4))
            for b in range(len(HB)):
                gelu(b)

        @block.gpsimd
        def _(pool):
            pool.memset(share[:, :], 1.0 / PD).then_inc(share_set, 1)
            pool.memset(mhalf[:, :], -0.5).then_inc(cleared, 1)
            pool.memset(phalf[:, :], 0.5)
            pool.memset(wv[:, :, :, :], 0.0).then_inc(cleared, 1)
            pool.memset(wu[:, :, :], 0.0).then_inc(cleared, 1)
            pool.memset(sq[:, :, :, :, :], 0.0)
            pool.memset(kp[:, :, :, :], 0.0).then_inc(cleared, 1)
            pool.memset(e1[:, :, :, :, :], 0.0)
            pool.memset(pr[:, :, :, :, :], 0.0).then_inc(cleared, 1)
            pool.memset(pt[:, :, :, :], 0.0).then_inc(cleared, 1)
            pool.memset(vT[:, :, :, TOK:TOK + 1], 1.0).then_inc(cleared, 1)
            pool.memset(hb[:, :, :, :, :], 0.0).then_inc(cleared, 1)
            pool.wait_ge(cleared, 8)

            def ln1_root(g):
                n = tokens(g)
                pool.wait_ge(mv1_ready, g + 1)
                pool.tensor_scalar(var1[0:n, g:g + 1], mv1[0:n, g, 1:2], EPS_TOK, None,
                                   ALU.add).then_inc(var1_ready, 1)
                pool.wait_ge(var1_ready, g + 1)
                pool.tensor_tensor(rstd1[0:n, g:g + 1], var1[0:n, g:g + 1], mhalf[0:n, 0:1],
                                   ALU.pow).then_inc(rstd1_ready, 1)

            def ln2_root(g):
                n = tokens(g)
                pool.wait_ge(mv2_ready, g + 1)
                pool.tensor_scalar(var2[0:n, g:g + 1], mv2[0:n, g, 1:2], EPS_TOK, None,
                                   ALU.add).then_inc(var2_ready, 1)
                pool.wait_ge(var2_ready, g + 1)
                pool.tensor_tensor(rstd2[0:n, g:g + 1], var2[0:n, g:g + 1], mhalf[0:n, 0:1],
                                   ALU.pow).then_inc(rstd2_ready, 1)

            def keep_h(g):
                n = tokens(g)
                pool.wait_ge(n_ready, g + 1)
                pool.tensor_tensor(z[0:n, g, :], n2[0:n, g % NN, :], g2row[0:n, :], ALU.mult).then_inc(rmul_ready, 1)
                pool.wait_ge(rmul_ready, g + 1)
                pool.tensor_tensor(z[0:n, g, :], z[0:n, g, :], b2row[0:n, :], ALU.add).then_inc(r_ready, 1)

            def qk_root(g):
                ni = images(g)
                pool.wait_ge(nsq_ready, g + 1)
                pool.tensor_tensor(rn[:, g, :, 0:ni], nsq[:, g, :, 0:ni],
                                   mhalf[:, :].rearrange("p (j i) -> p j i", j=4)[:, :, 0:ni],
                                   ALU.pow).then_inc(rn_ready, 1)
                pool.wait_ge(rn_ready, g + 1)
                pool.tensor_tensor(rqt[:, g, :, 0:ni], rn[:, g, 0:2, 0:ni],
                                   tempc[:, :].unsqueeze(2).broadcast_to([128, 2, ni]),
                                   ALU.mult).then_inc(rqt_ready, 1)

            def ln3_root(g):
                n = tokens(g)
                pool.wait_ge(mv3_ready, g + 1)
                pool.tensor_scalar(pw3[0:n, g, 0:1], mv3[0:n, g, 1:2], EPS_LN, None, ALU.add)
                pool.tensor_scalar(pw3[0:n, g, 1:2], mv3[0:n, g, 1:2], float(D), None,
                                   ALU.mult).then_inc(pw3_ready, 1)
                pool.wait_ge(pw3_ready, g + 1)
                pool.tensor_tensor(r3[0:n, g, 0:1], pw3[0:n, g, 0:1], mhalf[0:n, 0:1], ALU.pow)
                pool.tensor_tensor(r3[0:n, g, 1:2], pw3[0:n, g, 1:2], phalf[0:n, 0:1],
                                   ALU.pow).then_inc(r3_ready, 1)

            def ln4_root(g):
                n = tokens(g)
                pool.wait_ge(mv4_ready, g + 1)
                pool.tensor_scalar(var4[0:n, g:g + 1], mv4[0:n, g, 1:2], EPS_LN, None,
                                   ALU.add).then_inc(var4_ready, 1)
                pool.wait_ge(var4_ready, g + 1)
                pool.tensor_tensor(rstd4[0:n, g:g + 1], var4[0:n, g:g + 1], mhalf[0:n, 0:1],
                                   ALU.pow).then_inc(rstd4_ready, 1)

            ln1_root(0)
            for g in range(NG):
                if g + 1 < NG:
                    ln1_root(g + 1)
                ln2_root(g)
                if g == 1:
                    pool.wait_ge(rows_in, 48)
                    pool.tensor_tensor(b2row[:, :], b2row[:, :], bprow[:, :], ALU.add).then_inc(rowsum_ready, 1)
                    pool.wait_ge(rowsum_ready, 1)
                if g >= 1:
                    keep_h(g - 1)
            keep_h(NG - 1)
            pool.wait_ge(attn_in, 32)
            pool.wait_ge(sp_sum, 1)
            pool.tensor_tensor(spe[:, :, :], spn[:, :, :],
                               phalf[0:F, :].rearrange("p (f q) -> p f q", f=2), ALU.pow).then_inc(sp_root, 1)
            for s in range(NG + 4):
                if s < NG:
                    qk_root(s)
                if s >= 4:
                    ln3_root(s - 4)
            for g in range(NG):
                ln4_root(g)


def constants():
    token = np.arange(128) // TOK
    imgsel = (token[:, None] == np.arange(GI)[None, :]).astype(np.float32)
    slot = np.arange(GI * SL) // SL
    negmask = np.where(token[:, None] == slot[None, :], 0.0, NEG).astype(np.float32)
    unused = (np.arange(128) % 32 >= DH).astype(np.float32)
    pads = np.stack([unused, unused * np.float32(NEG)], axis=1).astype(np.float32)
    return {"ident": np.eye(128, dtype=np.float32), "imgsel": imgsel, "negmask": negmask, "pads": pads}


def kernel(**inputs):
    import concourse.bacc as _bacc
    from concourse.bass_utils import run_bass_kernel_spmd as _run

    nc = _bacc.Bacc("TRN2", target_bir_lowering=False, num_devices=1)
    arrays, args = {}, []
    w = {k.removeprefix("L0_"): np.asarray(v) for k, v in inputs.items()}
    patches = (w["x"].reshape(B, CH, SIDE, PATCH, SIDE, PATCH).transpose(0, 2, 4, 3, 5, 1)
               .reshape(NTOK, PD))
    arrays["in_x"] = patches
    arrays["in_x_t"] = np.concatenate(
        [patches[g * GI * TOK:g * GI * TOK + tokens(g)].reshape(tokens(g), KC, 128).transpose(2, 1, 0)
         .reshape(128, KC * tokens(g)) for g in range(NG)], axis=1)
    arrays["in_w_tok"] = w["tok_W_proj"]
    arrays["in_ln1_g"] = w["tok_ln1_g"].reshape(KC, 128).T
    arrays["in_ln1_b"] = w["tok_ln1_b"].reshape(KC, 128).T
    arrays["in_ln2_g"] = w["tok_ln2_g"]
    arrays["in_ln2_b"] = w["tok_ln2_b"]
    arrays["in_g2col"] = w["tok_ln2_g"].reshape(2, F).T
    arrays["in_b2col"] = w["tok_ln2_b"].reshape(2, F).T
    arrays["in_w_qkv"] = w["attn_W_qkv"]
    arrays["in_w_proj"] = w["attn_W_proj"]
    arrays["in_b_proj"] = w["attn_b_proj"]
    arrays["in_temp"] = np.repeat(w["attn_temp"].reshape(2, 4).T, 32, axis=0)
    arrays["in_slots"] = w["ffn_slot_params"]
    arrays["in_scale"] = w["ffn_scale"].reshape(1, 1)
    arrays["in_w_down"] = w["ffn_W_down"].reshape(NE, 2, F, HID).transpose(2, 1, 0, 3).reshape(F, 2, NE * HID)
    arrays["in_b_down"] = np.pad(w["ffn_b_down"].reshape(2, 4, HID), ((0, 0), (0, 0), (0, 32 - HID))).reshape(2, 128).T
    arrays["in_w_up"] = w["ffn_W_up"].reshape(2, 4, HID, D).transpose(1, 2, 0, 3)
    arrays["in_b_up"] = np.tile(np.repeat(w["ffn_b_up"], NP, axis=0), (GI, 1))
    arrays = {k: np.ascontiguousarray(v) for k, v in arrays.items()}
    for name, a in constants().items():
        arrays[f"const_{name}"] = a
    for name, a in arrays.items():
        args.append(nc.dram_tensor(name, a.shape, mybir.dt.from_np(a.dtype), kind="ExternalInput").ap())
    out = nc.dram_tensor("out_0", (B, TOK, D), F32, kind="ExternalOutput").ap()
    build(nc, *args, out)
    r = _run(nc, [arrays], core_ids=[0])
    return r.results[0]["out_0"]
```

```python
from contextlib import ExitStack

import numpy as np

import concourse.bass as bass
from concourse import mybir

F32 = mybir.dt.float32
ACT = mybir.ActivationFunctionType
ALU = mybir.AluOpType
AX = mybir.AxisListType

B, CH, IMG, PATCH = 32, 3, 96, 16
SIDE = IMG // PATCH
TOK = SIDE * SIDE
NTOK = B * TOK
D = 192
HEADS, DH = 8, D // 8
PD = CH * PATCH * PATCH
KC = PD // 128
GI = 3
NG = (B + GI - 1) // GI
F = D // 2
NE, NP = 8, 4
SL = NE * NP
HID = D // 8
HB = ((0, 4), (4, 8), (8, NG))
NEG = -1.0e30
EPS_TOK, EPS_LN, EPS_L2 = 1e-6, 1e-5, 1e-6


P1 = 9


def at(stage, g, first=0):
    if first <= g < NG:
        stage(g)


def images(g):
    return min(GI, B - g * GI)


def tokens(g):
    return images(g) * TOK


def build(nc, x, x_t, w_tok, ln1_g, ln1_b, ln2_g, ln2_b, g2col, b2col, w_qkv, w_proj, b_proj, temp, slots, scale,
          w_down, b_down, w_up, b_up, ident_h, imgsel_h, negmask_h, pads_h, out):
    ctx = ExitStack()
    with ctx:
        def sb(name, shape):
            return ctx.enter_context(nc.sbuf_tensor(name, shape, F32))

        def sem(name):
            return ctx.enter_context(nc.semaphore(name))

        ident = sb("ident", [128, 128])
        imgsel = sb("imgsel", [128, GI])
        negmask = sb("negmask", [128, GI * SL])
        pads = sb("pads", [128, 2])
        g1 = sb("g1", [128, KC])
        b1 = sb("b1", [128, KC])
        wt = sb("wt", [128, KC, D])
        wg = sb("wg", [128, KC, D])
        wc = sb("wc", [128, KC, D])
        bw = sb("bw", [128, D])
        share = sb("share", [128, 128])
        g2 = sb("g2", [F, 2])
        b2 = sb("b2", [F, 2])
        g2row = sb("g2row", [128, D])
        b2row = sb("b2row", [128, D])
        bprow = sb("bprow", [128, D])
        wraw = sb("wraw", [F, 2, HEADS, DH, 3])
        wqk = sb("wqk", [F, 2, 2, HEADS, DH])
        wv = sb("wv", [F, 2, HEADS, 32])
        wp = sb("wp", [F, 2, D])
        tempc = sb("tempc", [128, 2])
        spraw = sb("spraw", [F, 2, NE, NP])
        spsq = sb("spsq", [F, 2, NE, NP])
        spn = sb("spn", [F, 2, NP])
        spe = sb("spe", [F, 2, NP])
        sp3 = sb("sp3", [F, 2, GI, NE, NP])
        scl = sb("scl", [F, 1])
        wd = sb("wd", [F, 2, NE, HID])
        bd = sb("bd", [128, 2])
        wu = sb("wu", [128, 2, D])
        bu = sb("bu", [GI * SL, D])
        mhalf = sb("mhalf", [128, 12])
        phalf = sb("phalf", [128, 8])

        NB = 4
        xs = sb("xs", [128, NB, PD])
        st1 = sb("st1", [128, 2, 2, 6])
        mv1 = sb("mv1", [128, NG, 2])
        var1 = sb("var1", [128, NG])
        rstd1 = sb("rstd1", [128, NG])
        y1 = sb("y1", [128, NB, D])
        xT = sb("xT", [128, KC * NTOK])
        st2 = sb("st2", [128, 2, 6])
        mv2 = sb("mv2", [128, NG, 2])
        var2 = sb("var2", [128, NG])
        rstd2 = sb("rstd2", [128, NG])
        z = sb("z", [128, NG, D])
        hT = sb("hT", [F, 2, NTOK])
        NK = 3
        qp = sb("qp", [128, NK, HEADS, 32])
        km = sb("km", [128, NK, GI, D])
        sq = sb("sq", [128, 2, 2, HEADS, 32])
        nsq = sb("nsq", [128, NG, 4, GI])
        rn = sb("rn", [128, NG, 4, GI])
        rqt = sb("rqt", [128, NG, 2, GI])
        NS = 4
        rkb = sb("rkb", [128, 2, 2, GI, 32])
        sc = sb("sc", [128, 2, 2, GI, DH])
        e2 = sb("e2", [128, NS, 2, GI, DH])
        mx = sb("mx", [128, NS, 2, GI])
        pr = sb("pr", [128, NS, 2, GI, 32])
        pc = sb("pc", [128, 2, 2 * GI, 32])
        pt = sb("pt", [128, NS, 2 * GI, F])
        vT = sb("vT", [128, 2, B, TOK + 1])
        NY = 3
        rden = sb("rden", [F, NY, 2, GI])
        yT = sb("yT", [F, NY, 2, GI, TOK])
        st3 = sb("st3", [128, 2, 6])
        mv3 = sb("mv3", [128, NG, 2])
        pw3 = sb("pw3", [128, NG, 2])
        r3 = sb("r3", [128, NG, 2])
        nrm3 = sb("nrm3", [128, NG])
        inv3 = sb("inv3", [128, NG])
        xn = sb("xn", [128, NG, D])
        NX = 3
        xnT = sb("xnT", [F, NX, 2, GI * TOK])
        lm = sb("lm", [128, NX, GI * SL])
        mC = sb("mC", [128, NX])
        mD = sb("mD", [128, NX])
        eC = sb("eC", [128, NX, GI * SL])
        eD = sb("eD", [128, NX, GI * TOK])
        sC = sb("sC", [128, NG])
        sD = sb("sD", [128, NG])
        rC = sb("rC", [128, NG])
        rD = sb("rD", [128, NG])
        dm = sb("dm", [128, NX, GI * SL])
        cT = sb("cT", [GI * SL, NG, GI * TOK])
        xt = sb("xt", [F, 2, B, NE, NP])
        hb = sb("hb", [128, 2, B, NE, NP])
        NQ = 6
        yt = sb("yt", [GI * SL, NQ, D])
        z2 = sb("z2", [128, NQ, D])
        st4 = sb("st4", [128, 2, 6])
        mv4 = sb("mv4", [128, NG, 2])
        var4 = sb("var4", [128, NG])
        rstd4 = sb("rstd4", [128, NG])
        sh4 = sb("sh4", [128, NG])
        o4 = sb("o4", [128, NQ, D])

        ps = ctx.enter_context(nc.psum_tensor("ps", [128, 8, 512], F32))

        def csp():
            return ps[:, 0, 0:D]

        def bwp():
            return ps[:, 1, 0:D]

        def tokp(g):
            return ps[0:tokens(g), 6 + g % 2, 0:D]

        def htp(g):
            return ps[0:F, 5, 0:2 * GI * TOK].rearrange("p (f n) -> p f n", f=2)[:, :, 0:tokens(g)]

        def qkp(g):
            return ps[0:tokens(g), 0, 0:2 * D]

        def vp(g):
            return ps[:, 1, 0:2 * GI * TOK].rearrange("p (m n) -> p m n", m=2)[:, :, 0:tokens(g)]

        def nrmp(g):
            return ps[:, 2, 0:4 * GI].rearrange("p (j i) -> p j i", j=4)[:, :, 0:images(g)]

        def gramp(g):
            return ps[:, 3, 0:2 * GI * DH].rearrange("p (m i e) -> p m i e", m=2, i=GI)[:, :, 0:images(g), :]

        def yp(g):
            return ps[0:F, 4, 0:2 * GI * (TOK + 1)].rearrange("p (m i n) -> p m i n", m=2, i=GI)

        def prp(g):
            return ps[0:tokens(g), 4, 0:D]

        def xntp(g):
            return ps[0:F, 5, 0:2 * GI * TOK].rearrange("p (f n) -> p f n", f=2)[:, :, 0:tokens(g)]

        def lgp(g):
            return ps[0:tokens(g), 6, 0:images(g) * SL]

        def ltp(g):
            return ps[0:images(g) * SL, 6, 0:tokens(g)]

        def dp(g):
            return ps[0:tokens(g), 7, 0:images(g) * SL]

        def cp(g):
            return ps[0:images(g) * SL, 7, 128:128 + tokens(g)]

        def xtlp(g):
            return ps[0:F, 7, 0:2 * GI * SL].rearrange("p (f s) -> p f s", f=2)[:, :, 0:images(g) * SL]

        def hp(b, ni):
            return ps[:, b % 2, 0:2 * ni * NP].rearrange("p (e i s) -> p e i s", e=2, i=ni)

        def ytp(g):
            return ps[0:images(g) * SL, 2 + g % 2, 0:D]

        def yop(g):
            return ps[0:tokens(g), (4, 1)[g % 2], 0:D]

        x_in = [sem(f"x_in{g}") for g in range(NG)]
        xT_in = [sem(f"xT_in{g}") for g in range(NG)]
        ident_in = sem("ident_in")
        ln1_in = sem("ln1_in")
        wtok_in = sem("wtok_in")
        ln2_in = sem("ln2_in")
        wqkv_in = sem("wqkv_in")
        rows_in = sem("rows_in")
        masks_in = sem("masks_in")
        attn_in = sem("attn_in")
        slots_in = sem("slots_in")
        experts_in = sem("experts_in")
        out_done = [sem(f"out_done{i}") for i in range(NQ)]
        cleared = sem("cleared")
        wqk_ready = sem("wqk_ready")
        wv_ready = sem("wv_ready")
        rowsum_ready = sem("rowsum_ready")
        sp_sq = sem("sp_sq")
        sp_sum = sem("sp_sum")
        sp_root = sem("sp_root")
        sp_eps = sem("sp_eps")
        sp_inv = sem("sp_inv")
        sp_scaled = sem("sp_scaled")
        sp_ready = sem("sp_ready")
        share_set = sem("share_set")
        wg_ready = sem("wg_ready")
        csp_ready = sem("csp_ready")
        wc_ready = sem("wc_ready")
        bwp_ready = sem("bwp_ready")
        bw_ready = sem("bw_ready")
        st1_ready = sem("st1_ready")
        mv1_ready = sem("mv1_ready")
        var1_ready = sem("var1_ready")
        rstd1_ready = sem("rstd1_ready")
        y1_ready = sem("y1_ready")
        tokp_ready = sem("tokp_ready")
        st2_ready = sem("st2_ready")
        mv2_ready = sem("mv2_ready")
        var2_ready = sem("var2_ready")
        rstd2_ready = sem("rstd2_ready")
        n_ready = sem("n_ready")
        htp_ready = sem("htp_ready")
        hT_ready = sem("hT_ready")
        rmul_ready = sem("rmul_ready")
        r_ready = sem("r_ready")
        qkp_ready = sem("qkp_ready")
        sq_ready = sem("sq_ready")
        qk_ready = sem("qk_ready")
        nrmp_ready = sem("nrmp_ready")
        nsq_ready = sem("nsq_ready")
        rn_ready = sem("rn_ready")
        rqt_ready = sem("rqt_ready")
        gramp_ready = sem("gramp_ready")
        rkb_ready = sem("rkb_ready")
        sc_ready = sem("sc_ready")
        e2_scaled = sem("e2_scaled")
        mx_ready = sem("mx_ready")
        e2_ready = sem("e2_ready")
        pr_ready = sem("pr_ready")
        pc_ready = sem("pc_ready")
        pt_ready = sem("pt_ready")
        vp_ready = sem("vp_ready")
        v_ready = sem("v_ready")
        yp_ready = sem("yp_ready")
        rden_ready = sem("rden_ready")
        y_ready = sem("y_ready")
        prp_ready = sem("prp_ready")
        z_ready = sem("z_ready")
        st3_ready = sem("st3_ready")
        mv3_ready = sem("mv3_ready")
        pw3_ready = sem("pw3_ready")
        r3_ready = sem("r3_ready")
        nrm3_ready = sem("nrm3_ready")
        inv3_ready = sem("inv3_ready")
        h1_ready = sem("h1_ready")
        xn_ready = sem("xn_ready")
        xntp_ready = sem("xntp_ready")
        xnT_ready = sem("xnT_ready")
        lgp_ready = sem("lgp_ready")
        lm_ready = sem("lm_ready")
        mC_ready = sem("mC_ready")
        ltp_ready = sem("ltp_ready")
        mD_ready = sem("mD_ready")
        eC_ready = sem("eC_ready")
        eD_ready = sem("eD_ready")
        rD_ready = sem("rD_ready")
        eD_scaled = sem("eD_scaled")
        dcp_ready = sem("dcp_ready")
        dm_ready = sem("dm_ready")
        cT_ready = sem("cT_ready")
        xtlp_ready = sem("xtlp_ready")
        xt_ready = sem("xt_ready")
        hp_ready = sem("hp_ready")
        hb_ready = sem("hb_ready")
        ytp_ready = sem("ytp_ready")
        yt_ready = sem("yt_ready")
        yop_ready = sem("yop_ready")
        z2_ready = sem("z2_ready")
        st4_ready = sem("st4_ready")
        mv4_ready = sem("mv4_ready")
        var4_ready = sem("var4_ready")
        rstd4_ready = sem("rstd4_ready")
        sh4_ready = sem("sh4_ready")
        o4_ready = sem("o4_ready")

        block = ctx.enter_context(nc.Block())

        @block.sync
        def _(sp):
            def load_x(g):
                n = tokens(g)
                o = g * GI * TOK * KC
                sp.dma_start(xT[:, o:o + KC * n], x_t[:, o:o + KC * n]).then_inc(xT_in[g], 16)
                if g >= NB:
                    sp.wait_ge(st1_ready, g - NB + 1)
                sp.dma_start(xs[0:n, g % NB, :], x[g * GI * TOK:g * GI * TOK + n, :]).then_inc(x_in[g], 16)

            sp.dma_start(g1[:, :], ln1_g).then_inc(ln1_in, 16)
            sp.dma_start(b1[:, :], ln1_b).then_inc(ln1_in, 16)
            sp.dma_start(wt[:, :, :], w_tok.rearrange("(k p) e -> p k e", p=128)).then_inc(wtok_in, 16)
            load_x(0)
            sp.dma_start(ident[:, :], ident_h).then_inc(ident_in, 16)
            load_x(1)
            load_x(2)
            sp.dma_start(g2[:, :], g2col).then_inc(ln2_in, 16)
            sp.dma_start(b2[:, :], b2col).then_inc(ln2_in, 16)
            sp.dma_start(wraw[:, :, :, :, :].rearrange("p f h d j -> p f (h d j)"),
                         w_qkv.rearrange("(f p) n -> p f n", f=2)).then_inc(wqkv_in, 16)
            load_x(3)
            sp.dma_start(g2row[:, :], ln2_g.partition_broadcast(128)).then_inc(rows_in, 16)
            sp.dma_start(b2row[:, :], ln2_b.partition_broadcast(128)).then_inc(rows_in, 16)
            sp.dma_start(bprow[:, :], b_proj.partition_broadcast(128)).then_inc(rows_in, 16)
            sp.dma_start(imgsel[:, :], imgsel_h).then_inc(masks_in, 16)
            sp.dma_start(negmask[:, :], negmask_h).then_inc(masks_in, 16)
            sp.dma_start(pads[:, :], pads_h).then_inc(masks_in, 16)
            sp.dma_start(tempc[:, :], temp).then_inc(attn_in, 16)
            sp.dma_start(wp[:, :, :], w_proj.rearrange("(f p) n -> p f n", f=2)).then_inc(attn_in, 16)
            for g in range(4, NG):
                load_x(g)
            sp.dma_start(spraw[:, :, :, :].rearrange("p f n q -> p f (n q)"),
                         slots.rearrange("(f p) n q -> p f (n q)", f=2)).then_inc(slots_in, 16)
            sp.dma_start(scl[:, :], scale.broadcast_to([F, 1])).then_inc(slots_in, 16)
            sp.dma_start(wd[:, :, :, :].rearrange("p f n h -> p f (n h)"), w_down).then_inc(experts_in, 16)
            sp.dma_start(bd[:, :], b_down).then_inc(experts_in, 16)
            sp.dma_start(bu[:, :], b_up).then_inc(experts_in, 16)
            sp.wait_ge(cleared, 8)
            for j in range(4):
                sp.dma_start(wu[32 * j:32 * j + HID, :, :], w_up[j]).then_inc(experts_in, 16)

            ov = out.rearrange("b n d -> (b n) d")
            for g in range(NG):
                sp.wait_ge(o4_ready, g + 1)
                sp.dma_start(ov[g * GI * TOK:g * GI * TOK + tokens(g), :],
                             o4[0:tokens(g), g % NQ, :]).then_inc(out_done[g % NQ], 16)
            for i in range(NQ):
                sp.wait_ge(out_done[i], 16 * len(range(i, NG, NQ)))

        @block.tensor
        def _(pe):
            def offset():
                pe.wait_ge(ln1_in, 32)
                pe.wait_ge(wtok_in, 16)
                for kc in range(KC):
                    mm = pe.matmul(bwp(), b1[:, kc:kc + 1].broadcast_to([128, 128]), wt[:, kc, :],
                                   start=kc == 0, stop=kc == KC - 1)
                mm.then_inc(bwp_ready, 1)

            def column_means():
                pe.wait_ge(share_set, 1)
                for kc in range(KC):
                    pe.wait_ge(wg_ready, kc + 1)
                    mm = pe.matmul(csp(), share[:, :], wg[:, kc, :], start=kc == 0, stop=kc == KC - 1)
                mm.then_inc(csp_ready, 1)

            def token(g):
                n = tokens(g)
                o = g * GI * TOK * KC
                pe.wait_ge(xT_in[g], 16)
                if g >= 2:
                    pe.wait_ge(y1_ready, g - 1)
                for kc in range(KC):
                    mm = pe.matmul(tokp(g), xT[:, o + kc * n:o + (kc + 1) * n], wc[:, kc, :],
                                   start=kc == 0, stop=kc == KC - 1)
                mm.then_inc(tokp_ready, 1)

            def turn_h(g):
                pe.wait_ge(n_ready, g + 1)
                if g >= 1:
                    pe.wait_ge(hT_ready, g)
                for f in range(2):
                    mm = pe.transpose(htp(g)[:, f, :], z[0:tokens(g), g, f * F:(f + 1) * F],
                                      ident[0:tokens(g), 0:tokens(g)])
                mm.then_inc(htp_ready, 1)

            def qk(g):
                t0 = g * GI * TOK
                pe.wait_ge(hT_ready, g + 1)
                if g >= 1:
                    pe.wait_ge(qk_ready, g)
                for f in range(2):
                    mm = pe.matmul(qkp(g), hT[:, f, t0:t0 + tokens(g)],
                                   wqk[:, f, :, :, :].rearrange("p j h d -> p (j h d)"),
                                   start=f == 0, stop=f == 1)
                mm.then_inc(qkp_ready, 1)

            def norms(g):
                pe.wait_ge(sq_ready, g + 1)
                if g >= 1:
                    pe.wait_ge(nsq_ready, g)
                for j in range(2):
                    for m in range(2):
                        mm = pe.matmul(nrmp(g)[:, 2 * j + m, :],
                                       sq[0:tokens(g), g % 2, j, 4 * m:4 * m + 4, :].rearrange("p h d -> p (h d)"),
                                       imgsel[0:tokens(g), 0:images(g)], start=True, stop=True)
                mm.then_inc(nrmp_ready, 1)

            def gram(g):
                pe.wait_ge(qk_ready, g + 1)
                if g >= 1:
                    pe.wait_ge(e2_scaled, g)
                for m in range(2):
                    for j in range(4):
                        h = 4 * m + j
                        mm = pe.matmul(gramp(g)[32 * j:32 * j + 32, m, :, :], qp[0:tokens(g), g % NK, h, :],
                                       km[0:tokens(g), g % NK, 0:images(g), DH * h:DH * h + DH],
                                       start=True, stop=True, tile_position=(0, 32 * j))
                mm.then_inc(gramp_ready, 1)

            def values(g):
                t0 = g * GI * TOK
                if g >= 1:
                    pe.wait_ge(v_ready, g)
                for m in range(2):
                    for f in range(2):
                        mm = pe.matmul(vp(g)[:, m, :], wv[:, f, 4 * m:4 * m + 4, :].rearrange("p h d -> p (h d)"),
                                       hT[:, f, t0:t0 + tokens(g)], start=f == 0, stop=f == 1)
                mm.then_inc(vp_ready, 1)

            def mix(g):
                pe.wait_ge(pt_ready, g + 1)
                pe.wait_ge(v_ready, g + 1)
                if g >= 1:
                    pe.wait_ge(z_ready, g)
                for m in range(2):
                    for i in range(images(g)):
                        mm = pe.matmul(yp(g)[:, m, i, :], pt[:, g % NS, GI * m + i, 0:F],
                                       vT[:, m, g * GI + i, :], start=True, stop=True)
                mm.then_inc(yp_ready, 1)

            def project(g):
                pe.wait_ge(y_ready, g + 1)
                for m in range(2):
                    mm = pe.matmul(prp(g), yT[:, g % NY, m, 0:images(g), :].rearrange("p i n -> p (i n)"),
                                   wp[:, m, :], start=m == 0, stop=m == 1)
                mm.then_inc(prp_ready, 1)

            def turn_xn(g):
                pe.wait_ge(xn_ready, g + 1)
                if g == 0:
                    pe.wait_ge(hT_ready, NG)
                if g >= 1:
                    pe.wait_ge(xnT_ready, g)
                for f in range(2):
                    mm = pe.transpose(xntp(g)[:, f, :], xn[0:tokens(g), g, f * F:(f + 1) * F],
                                      ident[0:tokens(g), 0:tokens(g)])
                mm.then_inc(xntp_ready, 1)

            def logits(g):
                pe.wait_ge(xnT_ready, g + 1)
                if g == 0:
                    pe.wait_ge(sp_ready, 1)
                    pe.wait_ge(y1_ready, NG)
                if g >= 1:
                    pe.wait_ge(eD_ready, g)
                for f in range(2):
                    mm = pe.matmul(lgp(g), xnT[:, g % NX, f, 0:tokens(g)],
                                   sp3[:, f, 0:images(g), :, :].rearrange("p i n q -> p (i n q)"),
                                   start=f == 0, stop=f == 1)
                mm.then_inc(lgp_ready, 1)

            def turn_l(g):
                pe.wait_ge(lm_ready, g + 1)
                pe.transpose(ltp(g), lm[0:tokens(g), g % NX, 0:images(g) * SL],
                             ident[0:tokens(g), 0:tokens(g)]).then_inc(ltp_ready, 1)

            def turn_dc(g):
                n, s = tokens(g), images(g) * SL
                pe.wait_ge(eD_scaled, g + 1)
                pe.wait_ge(eC_ready, g + 1)
                if g >= 1:
                    pe.wait_ge(xt_ready, g)
                pe.transpose(dp(g), eD[0:s, g % NX, 0:n], ident[0:s, 0:s])
                pe.transpose(cp(g), eC[0:n, g % NX, 0:s], ident[0:n, 0:n]).then_inc(dcp_ready, 1)

            def slot_in(g):
                pe.wait_ge(dm_ready, g + 1)
                pe.wait_ge(cT_ready, g + 1)
                for f in range(2):
                    mm = pe.matmul(xtlp(g)[:, f, :], xn[0:tokens(g), g, f * F:(f + 1) * F],
                                   dm[0:tokens(g), g % NX, 0:images(g) * SL], start=True, stop=True)
                mm.then_inc(xtlp_ready, 1)

            def hidden(b):
                i0, i1 = HB[b][0] * GI, min(B, HB[b][1] * GI)
                pe.wait_ge(xt_ready, HB[b][1])
                if b >= 2:
                    pe.wait_ge(hb_ready, b - 1)
                for n in range(NE):
                    j = n % 4
                    for f in range(2):
                        mm = pe.matmul(hp(b, i1 - i0)[32 * j:32 * j + HID, n // 4, :, :], wd[:, f, n, :],
                                       xt[:, f, i0:i1, n, :], start=f == 0, stop=f == 1,
                                       tile_position=(0, 32 * j))
                mm.then_inc(hp_ready, 1)

            def slot_out(g):
                i0, ni = g * GI, images(g)
                pe.wait_ge(hb_ready, 1 + sum(g >= e for _, e in HB[:-1]))
                if g >= 2:
                    pe.wait_ge(yt_ready, g - 1)
                for e in range(2):
                    mm = pe.matmul(ytp(g), hb[:, e, i0:i0 + ni, :, :].rearrange("p i n q -> p (i n q)"),
                                   wu[:, e, :], start=e == 0, stop=e == 1)
                mm.then_inc(ytp_ready, 1)

            def combine(g):
                pe.wait_ge(yt_ready, g + 1)
                pe.wait_ge(cT_ready, g + 1)
                if g == 0:
                    pe.wait_ge(z_ready, NG)
                if g == 1:
                    pe.wait_ge(hb_ready, 2)
                if g >= 2:
                    pe.wait_ge(z2_ready, g - 1)
                pe.matmul(yop(g), cT[0:images(g) * SL, g, 0:tokens(g)], yt[0:images(g) * SL, g % NQ, :],
                          start=True, stop=True).then_inc(yop_ready, 1)

            offset()
            column_means()
            pe.wait_ge(wc_ready, 1)
            for g in range(P1):
                token(g)
                if g == 2:
                    pe.wait_ge(ident_in, 16)
                if g >= 2:
                    turn_h(g - 2)
            pe.wait_ge(wqk_ready, 2)
            pe.wait_ge(wv_ready, 2)
            pe.wait_ge(masks_in, 48)
            pe.wait_ge(attn_in, 32)
            pe.wait_ge(bw_ready, 1)
            for s in range(17):
                at(values, s - 2)
                at(project, s - 3)
                at(logits, s - 5)
                at(qk, s)
                at(turn_dc, s - 6)
                at(turn_l, s - 5)
                at(turn_h, s + P1 - 2 - 1, P1 - 2)
                at(token, s + P1 - 1, P1)
                at(gram, s - 1)
                at(mix, s - 2)
                at(turn_xn, s - 4)
                at(slot_in, s - 6)
                at(norms, s)
                if s == NG + 2:
                    pe.wait_ge(experts_in, 16 * (3 + 4))
                    pe.wait_ge(qk_ready, NG)
                    hidden(0)
                if s == NG + 3:
                    pe.wait_ge(v_ready, NG)
                    hidden(1)
            pe.wait_ge(nsq_ready, NG)
            pe.wait_ge(e2_scaled, NG)
            slot_out(0)
            slot_out(1)
            hidden(2)
            for g in range(2, NG):
                slot_out(g)
                combine(g - 2)
            combine(NG - 2)
            combine(NG - 1)

        @block.vector
        def _(dve):
            def token_weights():
                dve.wait_ge(ln1_in, 32)
                dve.wait_ge(wtok_in, 16)
                for kc in range(KC):
                    dve.tensor_scalar(wg[:, kc, :], wt[:, kc, :], g1[:, kc:kc + 1], None,
                                      ALU.mult).then_inc(wg_ready, 1)
                dve.wait_ge(wg_ready, KC)
                dve.wait_ge(csp_ready, 1)
                dve.tensor_tensor(wc[:, :, :], wg[:, :, :], csp().unsqueeze(1).broadcast_to([128, KC, D]),
                                  ALU.subtract).then_inc(wc_ready, 1)
                dve.wait_ge(bwp_ready, 1)
                dve.tensor_copy(bw[:, :], bwp()).then_inc(bw_ready, 1)
                dve.wait_ge(bw_ready, 1)

            def x_stats(g):
                n = tokens(g)
                dve.wait_ge(x_in[g], 16)
                if g >= 2:
                    dve.wait_ge(mv1_ready, g - 1)
                for h in range(2):
                    ins = dve.bn_stats(st1[0:n, g % 2, h, :], xs[0:n, g % NB, h * (PD // 2):(h + 1) * (PD // 2)])
                ins.then_inc(st1_ready, 1)

            def x_moments(g):
                n = tokens(g)
                dve.wait_ge(st1_ready, g + 1)
                dve.bn_aggr(mv1[0:n, g, :], st1[0:n, g % 2, :, :].rearrange("p h s -> p (h s)")).then_inc(mv1_ready, 1)

            def token_out(g):
                n = tokens(g)
                dve.wait_ge(tokp_ready, g + 1)
                dve.wait_ge(rstd1_ready, g + 1)
                if g >= NB:
                    dve.wait_ge(n_ready, g - NB + 1)
                dve.scalar_tensor_tensor(y1[0:n, g % NB, :], tokp(g), rstd1[0:n, g:g + 1], bw[0:n, :],
                                         ALU.mult, ALU.add).then_inc(y1_ready, 1)

            def token_stats(g):
                n = tokens(g)
                dve.wait_ge(y1_ready, g + 1)
                if g >= 2:
                    dve.wait_ge(mv2_ready, g - 1)
                dve.bn_stats(st2[0:n, g % 2, :], y1[0:n, g % NB, :]).then_inc(st2_ready, 1)

            def token_moments(g):
                n = tokens(g)
                dve.wait_ge(st2_ready, g + 1)
                dve.bn_aggr(mv2[0:n, g, :], st2[0:n, g % 2, :]).then_inc(mv2_ready, 1)

            def ln2_norm(g):
                n = tokens(g)
                dve.wait_ge(rstd2_ready, g + 1)
                dve.tensor_scalar(z[0:n, g, :], y1[0:n, g % NB, :], mv2[0:n, g, 0:1],
                                  rstd2[0:n, g:g + 1], ALU.subtract, ALU.mult).then_inc(n_ready, 1)

            def weights():
                dve.wait_ge(wqkv_in, 16)
                for f in range(2):
                    dve.tensor_copy(wqk[:, f, :, :, :],
                                    wraw[:, f, :, :, 0:2].rearrange("p h d j -> p j h d")).then_inc(wqk_ready, 1)
                dve.wait_ge(cleared, 8)
                for f in range(2):
                    dve.tensor_copy(wv[:, f, :, 0:DH], wraw[:, f, :, :, 2]).then_inc(wv_ready, 1)

            def slot_sums():
                dve.wait_ge(slots_in, 32)
                dve.tensor_tensor(spsq[:, :, :, :], spraw[:, :, :, :], spraw[:, :, :, :],
                                  ALU.mult).then_inc(sp_sq, 1)
                dve.wait_ge(sp_sq, 1)
                dve.tensor_reduce(spn[:, :, :], spsq[:, :, :, :].rearrange("p f n q -> p f q n"),
                                  AX.X, ALU.add).then_inc(sp_sum, 1)

            def slot_scale():
                dve.wait_ge(sp_root, 1)
                dve.tensor_scalar(spn[:, :, :], spe[:, :, :], EPS_L2, None, ALU.add).then_inc(sp_eps, 1)
                dve.wait_ge(sp_eps, 1)
                dve.reciprocal(spe[:, :, :], spn[:, :, :]).then_inc(sp_inv, 1)
                dve.wait_ge(sp_inv, 1)
                for f in range(2):
                    ins = dve.tensor_tensor(spsq[:, f, :, :], spraw[:, f, :, :],
                                            spe[:, f, :].unsqueeze(1).broadcast_to([F, NE, NP]), ALU.mult)
                ins.then_inc(sp_scaled, 1)
                dve.wait_ge(sp_scaled, 1)
                for i in range(GI):
                    ins = dve.tensor_scalar(sp3[:, :, i, :, :].rearrange("p f n q -> p f (n q)"),
                                            spsq[:, :, :, :].rearrange("p f n q -> p f (n q)"),
                                            scl[:, 0:1], None, ALU.mult)
                ins.then_inc(sp_ready, 1)

            def norm_sums(g):
                dve.wait_ge(nrmp_ready, g + 1)
                dve.tensor_scalar(nsq[:, g, :, 0:images(g)], nrmp(g), pads[:, 0:1], None,
                                  ALU.add).then_inc(nsq_ready, 1)

            def row_scales(g):
                ni = images(g)
                dve.wait_ge(rn_ready, g + 1)
                if g >= 2:
                    dve.wait_ge(sc_ready, g - 1)
                dve.transpose(rkb[:, g % 2, :, 0:ni, :],
                              rn[:, g, 2:4, 0:ni].unsqueeze(3).broadcast_to([128, 2, ni, 32])).then_inc(rkb_ready, 1)

            def scales(g):
                ni = images(g)
                dve.wait_ge(rkb_ready, g + 1)
                dve.wait_ge(rqt_ready, g + 1)
                if g >= 2:
                    dve.wait_ge(e2_scaled, g - 1)
                dve.tensor_tensor(sc[:, g % 2, :, 0:ni, :], rkb[:, g % 2, :, 0:ni, 0:DH],
                                  rqt[:, g, :, 0:ni].unsqueeze(3).broadcast_to([128, 2, ni, DH]),
                                  ALU.mult).then_inc(sc_ready, 1)

            def scores(g):
                ni = images(g)
                dve.wait_ge(gramp_ready, g + 1)
                dve.wait_ge(sc_ready, g + 1)
                if g >= NS:
                    dve.wait_ge(pr_ready, g - NS + 1)
                dve.tensor_tensor(e2[:, g % NS, :, 0:ni, :], gramp(g), sc[:, g % 2, :, 0:ni, :],
                                  ALU.mult).then_inc(e2_scaled, 1)

            def score_max(g):
                ni = images(g)
                dve.wait_ge(e2_scaled, g + 1)
                dve.tensor_reduce(mx[:, g % NS, :, 0:ni], e2[:, g % NS, :, 0:ni, :], AX.X, ALU.max).then_inc(mx_ready, 1)

            def score_shift(g):
                ni = images(g)
                s = g % NS
                v = e2[:, s, :, 0:ni, :]
                dve.wait_ge(mx_ready, g + 1)
                dve.tensor_tensor(v, v, mx[:, s, :, 0:ni].unsqueeze(3).broadcast_to([128, 2, ni, DH]),
                                  ALU.subtract).then_inc(e2_ready, 1)

            def turn_p(g):
                dve.wait_ge(pr_ready, g + 1)
                if g >= 2:
                    dve.wait_ge(pt_ready, g - 1)
                dve.transpose(pc[:, g % 2, :, :].rearrange("p b d -> p (b d)"),
                              pr[:, g % NS, :, :, :].rearrange("p m i e -> p (m i e)")).then_inc(pc_ready, 1)

            def y_sums(g):
                ni = images(g)
                dve.wait_ge(yp_ready, g + 1)
                if g >= NY:
                    dve.wait_ge(y_ready, g - NY + 1)
                dve.reciprocal(rden[:, g % NY, :, 0:ni], yp(g)[:, :, 0:ni, TOK]).then_inc(rden_ready, 1)

            def y_norm(g):
                ni = images(g)
                if g >= NY:
                    dve.wait_ge(prp_ready, g - NY + 1)
                dve.wait_ge(rden_ready, g + 1)
                dve.tensor_tensor(yT[:, g % NY, :, 0:ni, :], yp(g)[:, :, 0:ni, 0:TOK],
                                  rden[:, g % NY, :, 0:ni].unsqueeze(3).broadcast_to([F, 2, ni, TOK]),
                                  ALU.mult).then_inc(y_ready, 1)

            def residual(g):
                n = tokens(g)
                dve.wait_ge(prp_ready, g + 1)
                dve.wait_ge(r_ready, g + 1)
                dve.tensor_tensor(z[0:n, g, :], prp(g), z[0:n, g, :], ALU.add).then_inc(z_ready, 1)

            def residual_stats(g):
                n = tokens(g)
                dve.wait_ge(z_ready, g + 1)
                if g >= 2:
                    dve.wait_ge(mv3_ready, g - 1)
                dve.bn_stats(st3[0:n, g % 2, :], z[0:n, g, :]).then_inc(st3_ready, 1)

            def residual_moments(g):
                n = tokens(g)
                dve.wait_ge(st3_ready, g + 1)
                dve.bn_aggr(mv3[0:n, g, :], st3[0:n, g % 2, :]).then_inc(mv3_ready, 1)

            def h1_length(g):
                n = tokens(g)
                dve.wait_ge(r3_ready, g + 1)
                dve.tensor_scalar(nrm3[0:n, g:g + 1], r3[0:n, g, 0:1], r3[0:n, g, 1:2], EPS_L2,
                                  ALU.mult, ALU.add).then_inc(nrm3_ready, 1)

            def h1_inverse(g):
                n = tokens(g)
                dve.wait_ge(nrm3_ready, g + 1)
                dve.reciprocal(inv3[0:n, g:g + 1], nrm3[0:n, g:g + 1]).then_inc(inv3_ready, 1)

            def h1(g):
                n = tokens(g)
                dve.wait_ge(r3_ready, g + 1)
                dve.tensor_scalar(z[0:n, g, :], z[0:n, g, :], mv3[0:n, g, 0:1], r3[0:n, g, 0:1],
                                  ALU.subtract, ALU.mult).then_inc(h1_ready, 1)

            def unit_h1(g):
                n = tokens(g)
                dve.wait_ge(h1_ready, g + 1)
                dve.wait_ge(inv3_ready, g + 1)
                dve.tensor_scalar(xn[0:n, g, :], z[0:n, g, :], inv3[0:n, g:g + 1], None,
                                  ALU.mult).then_inc(xn_ready, 1)

            def mask_logits(g):
                n, s = tokens(g), images(g) * SL
                dve.wait_ge(lgp_ready, g + 1)
                if g >= NX:
                    dve.wait_ge(eC_ready, g - NX + 1)
                    dve.wait_ge(ltp_ready, g - NX + 1)
                dve.tensor_tensor(lm[0:n, g % NX, 0:s], lgp(g), negmask[0:n, 0:s], ALU.add).then_inc(lm_ready, 1)

            def max_c(g):
                n, s = tokens(g), images(g) * SL
                if g >= NX:
                    dve.wait_ge(eC_ready, g - NX + 1)
                dve.wait_ge(lm_ready, g + 1)
                dve.tensor_reduce(mC[0:n, g % NX:g % NX + 1], lm[0:n, g % NX, 0:s], AX.X, ALU.max,
                                  negate=True).then_inc(mC_ready, 1)

            def max_d(g):
                s = images(g) * SL
                dve.wait_ge(ltp_ready, g + 1)
                if g >= NX:
                    dve.wait_ge(eD_ready, g - NX + 1)
                dve.tensor_reduce(mD[0:s, g % NX:g % NX + 1], ltp(g), AX.X, ALU.max,
                                  negate=True).then_inc(mD_ready, 1)

            def invert_sums(g):
                n, s = tokens(g), images(g) * SL
                dve.wait_ge(eD_ready, g + 1)
                dve.wait_ge(eC_ready, g + 1)
                dve.reciprocal(rC[0:n, g:g + 1], sC[0:n, g:g + 1])
                dve.reciprocal(rD[0:s, g:g + 1], sD[0:s, g:g + 1]).then_inc(rD_ready, 1)

            def scale_d(g):
                n, s = tokens(g), images(g) * SL
                dve.wait_ge(rD_ready, g + 1)
                dve.tensor_scalar(eD[0:s, g % NX, 0:n], eD[0:s, g % NX, 0:n], rD[0:s, g:g + 1], None,
                                  ALU.mult).then_inc(eD_scaled, 1)

            def take_d(g):
                n, s = tokens(g), images(g) * SL
                dve.wait_ge(dcp_ready, g + 1)
                if g >= NX:
                    dve.wait_ge(xtlp_ready, g - NX + 1)
                dve.tensor_copy(dm[0:n, g % NX, 0:s], dp(g)).then_inc(dm_ready, 1)

            def slot_bias(g):
                s = images(g) * SL
                dve.wait_ge(ytp_ready, g + 1)
                if g >= NQ:
                    dve.wait_ge(yop_ready, g - NQ + 1)
                dve.tensor_tensor(yt[0:s, g % NQ, :], ytp(g), bu[0:s, :], ALU.add).then_inc(yt_ready, 1)

            def last_residual(g):
                n = tokens(g)
                dve.wait_ge(yop_ready, g + 1)
                if g >= NQ:
                    dve.wait_ge(o4_ready, g - NQ + 1)
                dve.scalar_tensor_tensor(z2[0:n, g % NQ, :], yop(g), rC[0:n, g:g + 1], z[0:n, g, :],
                                         ALU.mult, ALU.add).then_inc(z2_ready, 1)

            def last_stats(g):
                n = tokens(g)
                dve.wait_ge(z2_ready, g + 1)
                if g >= 2:
                    dve.wait_ge(mv4_ready, g - 1)
                dve.bn_stats(st4[0:n, g % 2, :], z2[0:n, g % NQ, :]).then_inc(st4_ready, 1)

            def last_moments(g):
                n = tokens(g)
                dve.wait_ge(st4_ready, g + 1)
                dve.bn_aggr(mv4[0:n, g, :], st4[0:n, g % 2, :]).then_inc(mv4_ready, 1)

            def last_shift(g):
                n = tokens(g)
                dve.wait_ge(rstd4_ready, g + 1)
                dve.scalar_tensor_tensor(sh4[0:n, g:g + 1], mv4[0:n, g, 0:1], -1.0, rstd4[0:n, g:g + 1],
                                         ALU.mult, ALU.mult).then_inc(sh4_ready, 1)

            token_weights()
            x_stats(0)
            x_moments(0)
            for s in range(P1):
                at(x_stats, s + 1)
                at(x_moments, s + 1)
                token_out(s)
                token_stats(s)
                at(ln2_norm, s - 1)
                token_moments(s)
                if s == 2:
                    weights()
            ln2_norm(P1 - 1)
            slot_sums()
            for s in range(16):
                if s == 4:
                    slot_scale()
                at(x_stats, s + P1 + 1, P1 + 1)
                at(max_c, s - 5)
                at(token_stats, s + P1 - 2, P1)
                at(unit_h1, s - 4)
                at(row_scales, s - 1)
                at(max_d, s - 5)
                at(token_moments, s + P1 - 2, P1)
                at(scales, s - 1)
                at(x_moments, s + P1 + 1, P1 + 1)
                at(y_sums, s - 2)
                at(scores, s - 1)
                at(token_out, s + P1 - 1, P1)
                at(y_norm, s - 2)
                at(score_max, s - 1)
                at(norm_sums, s)
                at(invert_sums, s - 5)
                at(score_shift, s - 1)
                at(scale_d, s - 5)
                at(h1_length, s - 3)
                at(h1, s - 3)
                at(turn_p, s - 1)
                at(h1_inverse, s - 3)
                at(residual, s - 2)
                at(mask_logits, s - 4)
                at(residual_stats, s - 2)
                at(take_d, s - 5)
                at(ln2_norm, s + P1 - 2, P1)
                at(residual_moments, s - 2)
            slot_bias(0)
            slot_bias(1)
            for g in range(2, NG + 4):
                at(last_residual, g - 2)
                at(last_moments, g - 3)
                at(slot_bias, g)
                at(last_stats, g - 2)
                at(last_shift, g - 4)

        @block.scalar
        def _(act):
            def take_h(g):
                t0 = g * GI * TOK
                act.wait_ge(htp_ready, g + 1)
                for f in range(2):
                    ins = act.activation(hT[:, f, t0:t0 + tokens(g)], htp(g)[:, f, :], ACT.Identity,
                                         bias=b2[:, f:f + 1], scale=g2[:, f:f + 1])
                ins.then_inc(hT_ready, 1)

            def square(g):
                n = tokens(g)
                act.wait_ge(qkp_ready, g + 1)
                if g >= 2:
                    act.wait_ge(nrmp_ready, g - 1)
                p = qkp(g).rearrange("p (j h d) -> p (j h) d", j=2, h=HEADS)
                act.activation(sq[0:n, g % 2, :, :, 0:DH].rearrange("p j h d -> p (j h) d"), p,
                               ACT.Square).then_inc(sq_ready, 1)

            def take_qk(g):
                n, ni = tokens(g), images(g)
                act.wait_ge(qkp_ready, g + 1)
                if g >= NK:
                    act.wait_ge(gramp_ready, g - NK + 1)
                p = qkp(g).rearrange("p (j h d) -> p (j h) d", j=2, h=HEADS)
                for i in range(ni):
                    act.activation(km[0:n, g % NK, i, :], qkp(g)[:, D:2 * D], ACT.Copy,
                                   scale=imgsel[0:n, i:i + 1])
                act.activation(qp[0:n, g % NK, :, 0:DH], p[:, 0:HEADS, :], ACT.Copy).then_inc(qk_ready, 1)

            def take_v(g):
                i0, ni = g * GI, images(g)
                act.wait_ge(vp_ready, g + 1)
                act.activation(vT[:, :, i0:i0 + ni, 0:TOK], vp(g).rearrange("p m (i n) -> p m i n", i=ni),
                               ACT.Copy).then_inc(v_ready, 1)

            def exp_e(g):
                ni = images(g)
                act.wait_ge(e2_ready, g + 1)
                if g >= NS:
                    act.wait_ge(pc_ready, g - NS + 1)
                act.activation(pr[:, g % NS, :, 0:ni, 0:DH], e2[:, g % NS, :, 0:ni, :], ACT.Exp,
                               bias=pads[:, 1:2]).then_inc(pr_ready, 1)

            def place_p(g):
                act.wait_ge(pc_ready, g + 1)
                if g >= NS:
                    act.wait_ge(yp_ready, g - NS + 1)
                for j in range(4):
                    r = slice(32 * j, 32 * j + 32)
                    ins = act.activation(pt[r, g % NS, :, DH * j:DH * j + DH], pc[r, g % 2, :, 0:DH], ACT.Copy)
                ins.then_inc(pt_ready, 1)

            def take_xn(g):
                act.wait_ge(xntp_ready, g + 1)
                if g >= NX:
                    act.wait_ge(lgp_ready, g - NX + 1)
                act.activation(xnT[:, g % NX, :, 0:tokens(g)], xntp(g), ACT.Copy).then_inc(xnT_ready, 1)

            def exp_c(g):
                n, s = tokens(g), images(g) * SL
                act.wait_ge(mC_ready, g + 1)
                if g >= NX:
                    act.wait_ge(dcp_ready, g - NX + 1)
                act.activation(eC[0:n, g % NX, 0:s], lm[0:n, g % NX, 0:s], ACT.Exp,
                               bias=mC[0:n, g % NX:g % NX + 1], accum_out=sC[0:n, g:g + 1]).then_inc(eC_ready, 1)

            def exp_d(g):
                n, s = tokens(g), images(g) * SL
                act.wait_ge(mD_ready, g + 1)
                act.activation(eD[0:s, g % NX, 0:n], ltp(g), ACT.Exp,
                               bias=mD[0:s, g % NX:g % NX + 1], accum_out=sD[0:s, g:g + 1]).then_inc(eD_ready, 1)

            def take_c(g):
                n, s = tokens(g), images(g) * SL
                act.wait_ge(dcp_ready, g + 1)
                act.wait_ge(dm_ready, g + 1)
                act.activation(cT[0:s, g, 0:n], cp(g), ACT.Copy).then_inc(cT_ready, 1)

            def take_slots(g):
                i0, ni = g * GI, images(g)
                act.wait_ge(xtlp_ready, g + 1)
                act.activation(xt[:, :, i0:i0 + ni, :, :].rearrange("p f i n q -> p f (i n q)"),
                               xtlp(g), ACT.Copy).then_inc(xt_ready, 1)

            def gelu(b):
                i0, i1 = HB[b][0] * GI, min(B, HB[b][1] * GI)
                act.wait_ge(hp_ready, b + 1)
                for n in range(NE):
                    r = slice(32 * (n % 4), 32 * (n % 4) + HID)
                    ins = act.activation(hb[r, n // 4, i0:i1, n, :], hp(b, i1 - i0)[r, n // 4, :, :],
                                         ACT.Gelu, bias=bd[r, n // 4:n // 4 + 1])
                ins.then_inc(hb_ready, 1)

            def last_norm(g):
                n = tokens(g)
                act.wait_ge(sh4_ready, g + 1)
                if g >= NQ:
                    act.wait_ge(out_done[g % NQ], 16 * (g // NQ))
                act.activation(o4[0:n, g % NQ, :], z2[0:n, g % NQ, :], ACT.Identity,
                               bias=sh4[0:n, g:g + 1], scale=rstd4[0:n, g:g + 1]).then_inc(o4_ready, 1)

            act.wait_ge(ln2_in, 32)
            for g in range(P1 - 2):
                take_h(g)
            act.wait_ge(masks_in, 48)
            act.wait_ge(cleared, 8)
            for s in range(17):
                at(exp_e, s - 2)
                at(take_v, s - 2)
                at(place_p, s - 2)
                at(square, s)
                at(take_c, s - 6)
                at(take_h, s + P1 - 2 - 1, P1 - 2)
                at(take_qk, s)
                at(exp_c, s - 5)
                at(exp_d, s - 5)
                at(take_xn, s - 4)
                at(take_slots, s - 6)
                if s == NG + 4:
                    act.wait_ge(experts_in, 16 * (3 + 4))
                    gelu(0)
            gelu(1)
            gelu(2)
            for g in range(NG):
                last_norm(g)

        @block.gpsimd
        def _(pool):
            pool.memset(share[:, :], 1.0 / PD).then_inc(share_set, 1)
            pool.memset(mhalf[:, :], -0.5).then_inc(cleared, 1)
            pool.memset(phalf[:, :], 0.5)
            pool.memset(wv[:, :, :, :], 0.0).then_inc(cleared, 1)
            pool.memset(wu[:, :, :], 0.0).then_inc(cleared, 1)
            pool.memset(sq[:, :, :, :, :], 0.0)
            pool.memset(qp[:, :, :, :], 0.0).then_inc(cleared, 1)
            pool.memset(pr[:, :, :, :, :], 0.0).then_inc(cleared, 1)
            pool.memset(pt[:, :, :, :], 0.0).then_inc(cleared, 1)
            pool.memset(vT[:, :, :, TOK:TOK + 1], 1.0).then_inc(cleared, 1)
            pool.memset(hb[:, :, :, :, :], 0.0).then_inc(cleared, 1)
            pool.wait_ge(cleared, 8)

            def ln1_var(g):
                n = tokens(g)
                pool.wait_ge(mv1_ready, g + 1)
                pool.tensor_scalar(var1[0:n, g:g + 1], mv1[0:n, g, 1:2], EPS_TOK, None,
                                   ALU.add).then_inc(var1_ready, 1)

            def ln1_root(g):
                n = tokens(g)
                pool.wait_ge(var1_ready, g + 1)
                pool.tensor_tensor(rstd1[0:n, g:g + 1], var1[0:n, g:g + 1], mhalf[0:n, 0:1],
                                   ALU.pow).then_inc(rstd1_ready, 1)

            def ln2_var(g):
                n = tokens(g)
                pool.wait_ge(mv2_ready, g + 1)
                pool.tensor_scalar(var2[0:n, g:g + 1], mv2[0:n, g, 1:2], EPS_TOK, None,
                                   ALU.add).then_inc(var2_ready, 1)

            def ln2_root(g):
                n = tokens(g)
                pool.wait_ge(var2_ready, g + 1)
                pool.tensor_tensor(rstd2[0:n, g:g + 1], var2[0:n, g:g + 1], mhalf[0:n, 0:1],
                                   ALU.pow).then_inc(rstd2_ready, 1)

            def keep_h_gain(g):
                n = tokens(g)
                pool.wait_ge(n_ready, g + 1)
                pool.wait_ge(htp_ready, g + 1)
                pool.tensor_tensor(z[0:n, g, :], z[0:n, g, :], g2row[0:n, :], ALU.mult).then_inc(rmul_ready, 1)

            def keep_h_offset(g):
                n = tokens(g)
                pool.wait_ge(rmul_ready, g + 1)
                pool.tensor_tensor(z[0:n, g, :], z[0:n, g, :], b2row[0:n, :], ALU.add).then_inc(r_ready, 1)

            def qk_root(g):
                ni = images(g)
                pool.wait_ge(nsq_ready, g + 1)
                pool.tensor_tensor(rn[:, g, :, 0:ni], nsq[:, g, :, 0:ni],
                                   mhalf[:, :].rearrange("p (j i) -> p j i", j=4)[:, :, 0:ni],
                                   ALU.pow).then_inc(rn_ready, 1)

            def q_scale(g):
                ni = images(g)
                pool.wait_ge(rn_ready, g + 1)
                pool.tensor_tensor(rqt[:, g, :, 0:ni], rn[:, g, 0:2, 0:ni],
                                   tempc[:, :].unsqueeze(2).broadcast_to([128, 2, ni]),
                                   ALU.mult).then_inc(rqt_ready, 1)

            def ln3_var(g):
                n = tokens(g)
                pool.wait_ge(mv3_ready, g + 1)
                pool.tensor_scalar(pw3[0:n, g, 0:1], mv3[0:n, g, 1:2], EPS_LN, None, ALU.add)
                pool.tensor_scalar(pw3[0:n, g, 1:2], mv3[0:n, g, 1:2], float(D), None,
                                   ALU.mult).then_inc(pw3_ready, 1)

            def ln3_root(g):
                n = tokens(g)
                pool.wait_ge(pw3_ready, g + 1)
                pool.tensor_tensor(r3[0:n, g, 0:1], pw3[0:n, g, 0:1], mhalf[0:n, 0:1], ALU.pow)
                pool.tensor_tensor(r3[0:n, g, 1:2], pw3[0:n, g, 1:2], phalf[0:n, 0:1],
                                   ALU.pow).then_inc(r3_ready, 1)

            def ln4_root(g):
                n = tokens(g)
                pool.wait_ge(mv4_ready, g + 1)
                pool.tensor_scalar(var4[0:n, g:g + 1], mv4[0:n, g, 1:2], EPS_LN, None,
                                   ALU.add).then_inc(var4_ready, 1)
                pool.wait_ge(var4_ready, g + 1)
                pool.tensor_tensor(rstd4[0:n, g:g + 1], var4[0:n, g:g + 1], mhalf[0:n, 0:1],
                                   ALU.pow).then_inc(rstd4_ready, 1)

            ln1_var(0)
            ln1_root(0)
            for g in range(P1):
                at(ln1_var, g + 1)
                at(ln1_root, g + 1)
                ln2_var(g)
                ln2_root(g)
            pool.wait_ge(rows_in, 48)
            pool.tensor_tensor(b2row[:, :], b2row[:, :], bprow[:, :], ALU.add).then_inc(rowsum_ready, 1)
            pool.wait_ge(attn_in, 32)
            pool.wait_ge(rowsum_ready, 1)
            for s in range(16):
                if s == 1:
                    pool.wait_ge(sp_sum, 1)
                    pool.tensor_tensor(spe[:, :, :], spn[:, :, :],
                                       phalf[0:F, :].rearrange("p (f q) -> p f q", f=2), ALU.pow).then_inc(sp_root, 1)
                at(keep_h_offset, s - 5)
                at(keep_h_gain, s - 2)
                at(ln2_root, s + P1 - 5, P1)
                at(ln1_root, s + P1 + 1 - 3, P1 + 1)
                at(qk_root, s - 3)
                at(ln1_var, s + P1 + 1, P1 + 1)
                at(ln2_var, s + P1 - 4, P1)
                at(q_scale, s - 3)
                at(ln3_var, s - 5)
                at(ln3_root, s - 5)
            for g in range(NG):
                ln4_root(g)


def constants():
    token = np.arange(128) // TOK
    imgsel = (token[:, None] == np.arange(GI)[None, :]).astype(np.float32)
    slot = np.arange(GI * SL) // SL
    negmask = np.where(token[:, None] == slot[None, :], 0.0, NEG).astype(np.float32)
    unused = (np.arange(128) % 32 >= DH).astype(np.float32)
    pads = np.stack([unused, unused * np.float32(NEG)], axis=1).astype(np.float32)
    return {"ident": np.eye(128, dtype=np.float32), "imgsel": imgsel, "negmask": negmask, "pads": pads}


def kernel(**inputs):
    import concourse.bacc as _bacc
    from concourse.bass_utils import run_bass_kernel_spmd as _run

    nc = _bacc.Bacc("TRN2", target_bir_lowering=False, num_devices=1)
    arrays, args = {}, []
    w = {k.removeprefix("L0_"): np.asarray(v) for k, v in inputs.items()}
    patches = (w["x"].reshape(B, CH, SIDE, PATCH, SIDE, PATCH).transpose(0, 2, 4, 3, 5, 1)
               .reshape(NTOK, PD))
    arrays["in_x"] = patches
    arrays["in_x_t"] = np.concatenate(
        [patches[g * GI * TOK:g * GI * TOK + tokens(g)].reshape(tokens(g), KC, 128).transpose(2, 1, 0)
         .reshape(128, KC * tokens(g)) for g in range(NG)], axis=1)
    arrays["in_w_tok"] = w["tok_W_proj"]
    arrays["in_ln1_g"] = w["tok_ln1_g"].reshape(KC, 128).T
    arrays["in_ln1_b"] = w["tok_ln1_b"].reshape(KC, 128).T
    arrays["in_ln2_g"] = w["tok_ln2_g"]
    arrays["in_ln2_b"] = w["tok_ln2_b"]
    arrays["in_g2col"] = w["tok_ln2_g"].reshape(2, F).T
    arrays["in_b2col"] = w["tok_ln2_b"].reshape(2, F).T
    arrays["in_w_qkv"] = w["attn_W_qkv"]
    arrays["in_w_proj"] = w["attn_W_proj"]
    arrays["in_b_proj"] = w["attn_b_proj"]
    arrays["in_temp"] = np.repeat(w["attn_temp"].reshape(2, 4).T, 32, axis=0)
    arrays["in_slots"] = w["ffn_slot_params"]
    arrays["in_scale"] = w["ffn_scale"].reshape(1, 1)
    arrays["in_w_down"] = w["ffn_W_down"].reshape(NE, 2, F, HID).transpose(2, 1, 0, 3).reshape(F, 2, NE * HID)
    arrays["in_b_down"] = np.pad(w["ffn_b_down"].reshape(2, 4, HID), ((0, 0), (0, 0), (0, 32 - HID))).reshape(2, 128).T
    arrays["in_w_up"] = w["ffn_W_up"].reshape(2, 4, HID, D).transpose(1, 2, 0, 3)
    arrays["in_b_up"] = np.tile(np.repeat(w["ffn_b_up"], NP, axis=0), (GI, 1))
    arrays = {k: np.ascontiguousarray(v) for k, v in arrays.items()}
    for name, a in constants().items():
        arrays[f"const_{name}"] = a
    for name, a in arrays.items():
        args.append(nc.dram_tensor(name, a.shape, mybir.dt.from_np(a.dtype), kind="ExternalInput").ap())
    out = nc.dram_tensor("out_0", (B, TOK, D), F32, kind="ExternalOutput").ap()
    build(nc, *args, out)
    r = _run(nc, [arrays], core_ids=[0])
    return r.results[0]["out_0"]
```
